# Optimizing a Trainium2 kernel written in Bass

```python
import numpy as np
import jax
import jax.numpy as jnp

def _softmax(x, axis=-1):
    return jax.nn.softmax(x, axis=axis)

def _gelu(x):
    return jax.nn.gelu(x, approximate=True)

def _silu(x):
    return jax.nn.silu(x)

def _sigmoid(x):
    return jax.nn.sigmoid(x)

def _layernorm(x, axis=-1, eps=1e-05):
    m = jnp.mean(x, axis=axis, keepdims=True)
    v = jnp.var(x, axis=axis, keepdims=True)
    return (x - m) / jnp.sqrt(v + eps)

def _scatter_add(tgt, idx, src, axis=0):
    return tgt.at[idx].add(src)

def _segment_sum(src, seg, n):
    return jax.ops.segment_sum(src, seg, n)
kernel_name = 'mk_cond_resid_d4_seqx_r8_ebb047'

def setup_inputs(seed: int=0):
    np.random.seed(seed)
    _w = jnp.asarray

    def _rec_inputs():
        import jax
        import jax.numpy as jnp
        _rk = jax.random.key(seed)
        x = -0.0003929 + 0.9999 * jax.random.normal(jax.random.fold_in(_rk, 1), (32, 128, 128), jnp.float32)
        _lenS = 128 - jax.random.randint(jax.random.fold_in(_rk, 7), (32,), 0, max(1, 128 // 4) + 1, jnp.int32)
        _lenS2 = 128 - jax.random.randint(jax.random.fold_in(_rk, 8), (32,), 0, max(1, 128 // 4) + 1, jnp.int32)
        cond_1024 = 0.00782532 + 1.00527 * jax.random.normal(jax.random.fold_in(_rk, 11), (32, 128), jnp.float32)
        fside_Bx1x1024x16_0 = 0.00222621 + 0.99962 * jax.random.normal(jax.random.fold_in(_rk, 12), (32, 1, 128, 16), jnp.float32)
        itok_B_14_1018 = jax.random.randint(jax.random.fold_in(_rk, 13), (32,), 14, 1019, jnp.int32)
        return (x, cond_1024, fside_Bx1x1024x16_0, itok_B_14_1018)
    x, cond_1024, fside_Bx1x1024x16_0, itok_B_14_1018 = _rec_inputs()

    def _L0_cond_setup():
        import jax, jax.numpy as jnp
        import numpy as np
        EPS = 1e-08
        key = jax.random.key(seed)
        ks = jax.random.split(key, 8)
        B, S, D, H = (8, 256, 128, 128)
        scale = 1.0 / np.sqrt(D)
        return {'input_seq': jax.random.normal(ks[0], (B, S, D), dtype=jnp.float32), 'initial_hidden': jax.random.normal(ks[1], (B, H), dtype=jnp.float32), 'W_f': jax.random.normal(ks[2], (H, D), dtype=jnp.float32) * scale, 'b_f': jnp.zeros((H,), dtype=jnp.float32), 'W_i': jax.random.normal(ks[3], (H, D), dtype=jnp.float32) * scale, 'b_i': jnp.zeros((H,), dtype=jnp.float32), 'W_h': jax.random.normal(ks[4], (H, D), dtype=jnp.float32) * scale, 'b_h': jnp.zeros((H,), dtype=jnp.float32)}
    _L0_cond_all = _L0_cond_setup()
    _L0_cond_in = {k: v for k, v in _L0_cond_all.items() if k in ('W_f', 'b_f', 'W_i', 'b_i', 'W_h', 'b_h')}
    del _L0_cond_all

    def _L1_cond_setup():
        import jax, jax.numpy as jnp
        import numpy as np
        D_MODEL = 128
        D_FF = 512
        N_EXPERTS = 8
        TOP_K = 2
        N_SHARED = 2
        B, T = (4, 256)
        key = jax.random.key(seed)
        ks = jax.random.split(key, 9)
        Hs = D_FF // 2
        Hr = D_FF // 4
        inp = {'x': jax.random.normal(ks[0], (B, T, D_MODEL), dtype=jnp.float32), 't_emb': jax.random.normal(ks[1], (B, D_MODEL), dtype=jnp.float32), 'W_router': 0.01 * jax.random.normal(ks[2], (N_EXPERTS, 2 * D_MODEL), dtype=jnp.float32), 'router_bias': jnp.zeros((N_EXPERTS,), dtype=jnp.float32), 's_w1': 0.02 * jax.random.normal(ks[3], (N_SHARED, Hs, D_MODEL), dtype=jnp.float32), 's_w3': 0.02 * jax.random.normal(ks[4], (N_SHARED, Hs, D_MODEL), dtype=jnp.float32), 's_w2': 0.02 * jax.random.normal(ks[5], (N_SHARED, D_MODEL, Hs), dtype=jnp.float32), 'r_w1': 0.02 * jax.random.normal(ks[6], (N_EXPERTS, Hr, D_MODEL), dtype=jnp.float32), 'r_w2': 0.02 * jax.random.normal(ks[7], (N_EXPERTS, D_MODEL, Hr), dtype=jnp.float32)}
        return inp
    _L1_cond_all = _L1_cond_setup()
    _L1_cond_in = {k: v for k, v in _L1_cond_all.items() if k in ('W_router', 'router_bias', 's_w1', 's_w3', 's_w2', 'r_w1', 'r_w2')}
    del _L1_cond_all

    def _L2_cond_setup():
        import jax, jax.numpy as jnp
        import numpy as np
        B, F_, IN, OUT, R = (32, 64, 128, 128, 16)
        key = jax.random.key(seed)
        ks = jax.random.split(key, 6)
        x = jax.random.normal(ks[0], (B, F_, IN), dtype=jnp.float32)
        u = jax.random.normal(ks[1], (B, 1, OUT, R), dtype=jnp.float32)
        v = jax.random.normal(ks[2], (B, 1, IN, R), dtype=jnp.float32)
        b = jax.random.normal(ks[3], (B, 1, OUT), dtype=jnp.float32)
        lim = 1.0 / np.sqrt(IN)
        W = jax.random.uniform(ks[4], (OUT, IN), minval=-lim, maxval=lim, dtype=jnp.float32)
        fc_bias = jax.random.uniform(ks[5], (OUT,), minval=-lim, maxval=lim, dtype=jnp.float32)
        return {'x': x, 'u': u, 'v': v, 'b': b, 'W': W, 'fc_bias': fc_bias}
    _L2_cond_all = _L2_cond_setup()
    _L2_cond_in = {k: v for k, v in _L2_cond_all.items() if k in ('W', 'fc_bias')}
    del _L2_cond_all

    def _L3_cond_setup():
        import jax, jax.numpy as jnp
        import numpy as np
        P_DROP = 0.2
        FORCE_NONZERO = True
        key = jax.random.key(seed)
        k1, k2, k3 = jax.random.split(key, 3)
        B, M, D = (128, 32, 128)
        z = jax.random.normal(k1, (B, M, D), dtype=jnp.float32)
        noise = jax.random.uniform(k2, (B, D), dtype=jnp.float32)
        fallback_idx = jax.random.randint(k3, (B,), 0, D, dtype=jnp.int64)
        return {'z': z, 'noise': noise, 'fallback_idx': fallback_idx}
    _L3_cond_all = _L3_cond_setup()
    _L3_cond_in = {k: v for k, v in _L3_cond_all.items() if k in ()}
    del _L3_cond_all
    return {'x': x, 'cond_1024': cond_1024, 'fside_Bx1x1024x16_0': fside_Bx1x1024x16_0, 'itok_B_14_1018': itok_B_14_1018, 'L0_cond_W_f': _L0_cond_in['W_f'], 'L0_cond_b_f': _L0_cond_in['b_f'], 'L0_cond_W_i': _L0_cond_in['W_i'], 'L0_cond_b_i': _L0_cond_in['b_i'], 'L0_cond_W_h': _L0_cond_in['W_h'], 'L0_cond_b_h': _L0_cond_in['b_h'], 'L1_cond_W_router': _L1_cond_in['W_router'], 'L1_cond_router_bias': _L1_cond_in['router_bias'], 'L1_cond_s_w1': _L1_cond_in['s_w1'], 'L1_cond_s_w3': _L1_cond_in['s_w3'], 'L1_cond_s_w2': _L1_cond_in['s_w2'], 'L1_cond_r_w1': _L1_cond_in['r_w1'], 'L1_cond_r_w2': _L1_cond_in['r_w2'], 'L2_cond_W': _L2_cond_in['W'], 'L2_cond_fc_bias': _L2_cond_in['fc_bias']}

def reference(x, cond_1024, fside_Bx1x1024x16_0, itok_B_14_1018, L0_cond_W_f, L0_cond_b_f, L0_cond_W_i, L0_cond_b_i, L0_cond_W_h, L0_cond_b_h, L1_cond_W_router, L1_cond_router_bias, L1_cond_s_w1, L1_cond_s_w3, L1_cond_s_w2, L1_cond_r_w1, L1_cond_r_w2, L2_cond_W, L2_cond_fc_bias):
    import jax
    import jax.numpy as jnp

    def _L0_cond_ref(input_seq, initial_hidden, W_f, b_f, W_i, b_i, W_h, b_h):
        import jax, jax.numpy as jnp
        import numpy as np
        EPS = 1e-08
        forget_gate = jax.nn.sigmoid(jnp.einsum('bsd,hd->bsh', input_seq, W_f) + b_f)
        input_gate = jax.nn.sigmoid(jnp.einsum('bsd,hd->bsh', input_seq, W_i) + b_i)
        gate_sum = forget_gate + input_gate + EPS
        forget_norm = forget_gate / gate_sum
        input_norm = input_gate / gate_sum
        candidate = jnp.einsum('bsd,hd->bsh', input_seq, W_h) + b_h
        new_info = input_norm * candidate
        log_ret = jnp.log(forget_norm + EPS)
        log_cumprod = jnp.cumsum(log_ret, axis=1)
        B, _, H = log_cumprod.shape
        padded = jnp.concatenate([jnp.zeros((B, 1, H), dtype=log_cumprod.dtype), log_cumprod], axis=1)
        scaling = jnp.exp(log_cumprod[:, -1:, :] - padded[:, :-1, :])
        hidden = jnp.cumsum(scaling * new_info, axis=1)
        hidden = hidden + jnp.exp(log_cumprod) * initial_hidden[:, None, :]
        return hidden

    def _L1_cond_ref(x, t_emb, W_router, router_bias, s_w1, s_w3, s_w2, r_w1, r_w2):
        import jax, jax.numpy as jnp
        import numpy as np
        D_MODEL = 128
        D_FF = 512
        N_EXPERTS = 8
        TOP_K = 2
        N_SHARED = 2
        B, T = (4, 256)
        Bn, Tn, C = x.shape
        N = Bn * Tn
        x_flat = x.reshape(N, C)
        t_flat = jnp.broadcast_to(t_emb[:, None, :], (Bn, Tn, C)).reshape(N, C)
        shared_out = jnp.zeros_like(x_flat)
        for e in range(N_SHARED):
            h = jax.nn.silu(x_flat @ s_w1[e].T) * (x_flat @ s_w3[e].T)
            shared_out = shared_out + h @ s_w2[e].T
        shared_out = shared_out / N_SHARED
        router_in = jnp.concatenate([x_flat, t_flat], axis=-1)
        s = jax.nn.sigmoid((router_in @ W_router.T).astype(jnp.float32))
        sel_scores = s + router_bias
        _, topk_idx = jax.lax.top_k(sel_scores, TOP_K)
        s_sel = jnp.take_along_axis(s, topk_idx, axis=1)
        denom = jnp.sum(s_sel, axis=1, keepdims=True)
        gates = jnp.where(denom > 1e-09, s_sel / (denom + 1e-09), 1.0 / TOP_K).astype(x.dtype)
        gates_full = jnp.sum(jax.nn.one_hot(topk_idx, N_EXPERTS, dtype=x.dtype) * gates[..., None], axis=1)
        routed_out = jnp.zeros_like(x_flat)
        for e in range(N_EXPERTS):
            h = jax.nn.gelu(x_flat @ r_w1[e].T, approximate=False)
            routed_out = routed_out + h @ r_w2[e].T * gates_full[:, e:e + 1]
        out = (shared_out + routed_out) / (N_SHARED + TOP_K)
        return out.reshape(Bn, Tn, C)

    def _L2_cond_ref(x, u, v, b, W, fc_bias):
        import jax, jax.numpy as jnp
        import numpy as np
        B, F_, IN, OUT, R = (32, 64, 128, 128, 16)
        inch = x.shape[-1]
        r = v.shape[-1]
        z1 = jnp.einsum('bfi,bir->bfr', x, v[:, 0]) / inch
        z = jnp.einsum('bfr,bor->bfo', z1, u[:, 0]) / r
        y = jnp.einsum('bfi,oi->bfo', x, W) + fc_bias + z + b
        return jax.nn.gelu(y, approximate=False)

    def _L3_cond_ref(z, noise, fallback_idx):
        import jax, jax.numpy as jnp
        import numpy as np
        P_DROP = 0.2
        FORCE_NONZERO = True
        mask = (noise < 1.0 - P_DROP).astype(z.dtype)
        if FORCE_NONZERO:
            B = mask.shape[0]
            all_zero = jnp.all(mask == 0, axis=1)
            rows = jnp.arange(B)
            picked = mask[rows, fallback_idx]
            mask = mask.at[rows, fallback_idx].set(jnp.where(all_zero, jnp.ones_like(picked), picked))
        return mask[:, None, :] * z
    x = x + _L0_cond_ref(x, cond_1024, L0_cond_W_f, L0_cond_b_f, L0_cond_W_i, L0_cond_b_i, L0_cond_W_h, L0_cond_b_h)
    x = x + _L1_cond_ref(x, cond_1024, L1_cond_W_router, L1_cond_router_bias, L1_cond_s_w1, L1_cond_s_w3, L1_cond_s_w2, L1_cond_r_w1, L1_cond_r_w2)
    x = x + _L2_cond_ref(x, fside_Bx1x1024x16_0, fside_Bx1x1024x16_0, cond_1024[:, None, :], L2_cond_W, L2_cond_fc_bias)
    x = x + _L3_cond_ref(x, cond_1024, itok_B_14_1018)
    return x

_drawn_inputs = setup_inputs


def setup_inputs(seed=0):
    import zlib

    import numpy as np

    out = dict(_drawn_inputs(seed))
    spreads = {'L0_cond_b_f': (0.0, 2.0),
     'L0_cond_b_i': (0.0, 2.0),
     'L0_cond_b_h': (0.0, 0.8),
     'L1_cond_router_bias': (0.0, 0.8)}
    factors = {'fside_Bx1x1024x16_0': 4.802,
     'L0_cond_W_f': 4.37,
     'L0_cond_W_i': 4.316,
     'L1_cond_W_router': 8.0,
     'L1_cond_s_w1': 8.0,
     'L1_cond_s_w3': 8.0,
     'L1_cond_s_w2': 8.0,
     'L1_cond_r_w1': 8.0,
     'L1_cond_r_w2': 8.0,
     'L2_cond_fc_bias': 2.754}
    for name, (base, spread) in spreads.items():
        noise = np.random.default_rng([zlib.crc32(name.encode()), seed]).standard_normal(out[name].shape)
        drawn = base * np.exp(spread * noise) if base else spread * noise
        out[name] = jnp.asarray(drawn.astype(out[name].dtype))
    for name, factor in factors.items():
        out[name] = (out[name] * factor).astype(out[name].dtype)
    return out
```

```python
import concourse.bass as bass
from concourse import mybir
from contextlib import ExitStack

B, S, D = 32, 128, 128
R = 16
E = 8
SHARED = 2
GB = 4
N = GB * S
GROUPS = B // GB
PAD = S + 1
EPS = 1e-8
KEEP = 0.8
BIG = 3.0e38
SU = SHARED * 2
WF, WI, WH = 0, 1, 2
W1, W3 = 3, 3 + SU
WR = 3 + 2 * SU
WL = WR + E
BLOCKS = WL + 1


class Step:

    def __init__(self, start, register=None, step=2):
        self.start, self.register, self.step = start, register, step

    def plus(self, n):
        return Step(self.start + n, self.register, self.step)

    @property
    def runs(self):
        return self.register is not None or 0 <= self.start < GROUPS

    @property
    def first(self):
        return self.register is None and self.start == 0

    @property
    def parity(self):
        return self.start % 2

    def count(self, per_group, k):
        if self.register is None:
            return self.start * per_group + k
        return self.register * (self.step * per_group) + (self.start * per_group + k)


def build(nc, xT, condT, fsT, fsR, itok, wfT, bf, wiT, bi, whT, bh, wrT, rbias, s1T, s3T, s2T, r1T, r2T, wlT, fcb,
          c_block, c_sel, c_eye, c_index, c_rank, outT):
    F32, F32R, I32 = mybir.dt.float32, mybir.dt.float32r, mybir.dt.int32
    ALU, ACT, AX = mybir.AluOpType, mybir.ActivationFunctionType, mybir.AxisListType

    with ExitStack() as ctx:
        def sb(name, shape, dt=F32):
            return ctx.enter_context(nc.sbuf_tensor(name, shape, dt))

        def sem(name):
            return ctx.enter_context(nc.semaphore(name))

        w_raw = sb("w_raw", [128, BLOCKS, 128])
        w_hi = sb("w_hi", [128, BLOCKS, 128], F32R)
        w_lo = sb("w_lo", [128, BLOCKS, 128], F32R)
        down = sb("down", [128, SU + E, 128])
        wr_raw = sb("wr_raw", [128, 2, E])
        wr_hi = sb("wr_hi", [128, E], F32R)
        wr_lo = sb("wr_lo", [128, E], F32R)
        cond = sb("cond", [128, B])
        biases = sb("biases", [128, 4])
        route_bias = sb("route_bias", [128, E])
        rank = sb("rank", [128, E])
        index = sb("index", [128, 2])
        block_mask = sb("block_mask", [128, N])
        sel_raw = sb("sel_raw", [128, E, 128])
        sel = sb("sel", [128, E, 128], F32R)
        eye_raw = sb("eye_raw", [128, 128])
        eye = sb("eye", [128, 128], F32R)
        eps_col = sb("eps_col", [128, 1])
        ones = sb("ones", [128, 128])
        scan_mask = sb("scan_mask", [128, GB * PAD])
        tok_i = sb("tok_i", [128, B], I32)
        tok_f = sb("tok_f", [128, B])
        keep = sb("keep", [128, B])
        all_zero = sb("all_zero", [128, B])
        hit_a = sb("hit_a", [128, B])
        hit_b = sb("hit_b", [128, B])
        gain = sb("gain", [128, B])
        bias2 = sb("bias2", [128, B])
        route_cond = sb("route_cond", [128, B * E])

        x_in = [sb(f"x_in{p}", [128, N]) for p in range(2)]
        x_hi = sb("x_hi", [128, N], F32R)
        x_lo = sb("x_lo", [128, N], F32R)
        forget = sb("forget", [128, N])
        inp = sb("inp", [128, N])
        cand = sb("cand", [128, N])
        gate_sum = sb("gate_sum", [128, N])
        log_sum = sb("log_sum", [128, N])
        inv_sum = sb("inv_sum", [128, N])
        forget_norm = sb("forget_norm", [128, N])
        input_norm = sb("input_norm", [128, N])
        new_info = sb("new_info", [128, N])
        log_ret = sb("log_ret", [128, GB * PAD])
        log_cum = sb("log_cum", [128, GB * PAD])
        log_scale = sb("log_scale", [128, N])
        scaling = sb("scaling", [128, N])
        retained = sb("retained", [128, N])
        scaled = sb("scaled", [128, GB * PAD])
        scaled_cum = sb("scaled_cum", [128, GB * PAD])
        hidden = sb("hidden", [128, N])
        x1 = [sb(f"x1_{p}", [128, N]) for p in range(2)]
        x1_hi = [sb(f"x1_hi{p}", [128, N], F32R) for p in range(2)]
        x1_lo = [sb(f"x1_lo{p}", [128, N], F32R) for p in range(2)]

        logits = sb("logits", [128, GB * E])
        score = sb("score", [128, GB * E])
        t8 = {n: sb(n, [128, GB, E]) for n in
              ("biased", "top1", "ranked1", "one1", "rest", "top2", "ranked2", "one2", "chosen", "kept", "even",
               "gate_a", "gate")}
        t1 = {n: sb(n, [128, GB]) for n in
              ("max1", "first1", "max2", "first2", "denom", "denom_eps", "inv_denom", "valid", "gain_valid",
               "fallback")}
        gate_parts = sb("gate_parts", [128, GB, 128], F32R)
        gates_T = sb("gates_T", [128, N], F32R)
        silu = [sb(f"silu{p}", [128, N]) for p in range(2)]
        h_shared = sb("h_shared", [128, SU, N])
        gelu = [sb(f"gelu{p}", [128, N]) for p in range(3)]
        h_gated = [sb(f"h_gated{p}", [128, N]) for p in range(3)]
        x2 = sb("x2", [128, N])
        x2_hi = sb("x2_hi", [128, N], F32R)
        x2_lo = sb("x2_lo", [128, N], F32R)

        v_in = sb("v_in", [128, GB * R])
        v_parts = sb("v_parts", [128, 2, GB * R], F32R)
        u_in = sb("u_in", [128, 128])
        z1 = sb("z1", [128, N])
        act2 = sb("act2", [128, N])
        x3 = sb("x3", [128, N])
        out_sb = sb("out_sb", [128, N])

        bank = [ctx.enter_context(nc.psum_tensor(f"bank{i}", [128, N], F32)) for i in range(8)]
        ACC, ROUTE, LOWRANK, LINEAR = bank[5], bank[6], bank[7], bank[4]
        GATE = (bank[3], bank[4])
        PAIRS = ((bank[3], bank[4]), (bank[7], bank[5]), (bank[0], bank[1]), (bank[2], bank[3]))

        w0_loaded, wup_loaded, down_loaded = sem("w0_loaded"), sem("wup_loaded"), sem("down_loaded")
        small_loaded, consts_loaded = sem("small_loaded"), sem("consts_loaded")
        x_loaded = [sem(f"x_loaded{p}") for p in range(2)]
        v_loaded, u_loaded, out_stored = sem("v_loaded"), sem("u_loaded"), sem("out_stored")
        w0_split, wup_split, consts_ready = sem("w0_split"), sem("wup_split"), sem("consts_ready")
        pads_ready, keep_ready, kept_counted = sem("pads_ready"), sem("keep_ready"), sem("kept_counted")
        setup_step, cond_routed, route_cond_ready = sem("setup_step"), sem("cond_routed"), sem("route_cond_ready")
        x_hi_ready, x_lo_ready, gates_mm = sem("x_hi_ready"), sem("x_lo_ready"), sem("gates_mm")
        forget_ready, inp_ready, cand_ready = sem("forget_ready"), sem("inp_ready"), sem("cand_ready")
        gate_sum_ready, log_sum_ready, inv_sum_ready = sem("gate_sum_ready"), sem("log_sum_ready"), sem("inv_sum_ready")
        forget_norm_ready, input_norm_ready = sem("forget_norm_ready"), sem("input_norm_ready")
        new_info_ready, log_ret_ready, log_cum_ready = sem("new_info_ready"), sem("log_ret_ready"), sem("log_cum_ready")
        log_scale_ready, scaling_ready, retained_ready = sem("log_scale_ready"), sem("scaling_ready"), sem("retained_ready")
        scaled_ready, scaled_cum_ready, hidden_ready = sem("scaled_ready"), sem("scaled_cum_ready"), sem("hidden_ready")
        x1_ready, x1_hi_ready, x1_lo_ready = sem("x1_ready"), sem("x1_hi_ready"), sem("x1_lo_ready")
        route_mm, logits_ready, score_ready = sem("route_mm"), sem("logits_ready"), sem("score_ready")
        gate_step, gate_parts_ready = sem("gate_step"), sem("gate_parts_ready")
        gates_T_mm, gates_T_ready = sem("gates_T_mm"), sem("gates_T_ready")
        shared_mm, silu_ready, h_shared_ready = sem("shared_mm"), sem("silu_ready"), sem("h_shared_ready")
        expert_mm, gate_mm, gelu_ready = sem("expert_mm"), sem("gate_mm"), sem("gelu_ready")
        h_gated_ready, down_mm = sem("h_gated_ready"), sem("down_mm")
        x2_ready, x2_hi_ready, x2_lo_ready = sem("x2_ready"), sem("x2_hi_ready"), sem("x2_lo_ready")
        v_hi_ready, v_lo_ready = sem("v_hi_ready"), sem("v_lo_ready")
        z1_mm, z1_ready, linear_mm, act2_ready = sem("z1_mm"), sem("z1_ready"), sem("linear_mm"), sem("act2_ready")
        x3_ready, out_ready = sem("x3_ready"), sem("out_ready")

        block = ctx.enter_context(nc.Block())

        GATE_STEPS = 24
        SETUP_STEPS = 11
        SMALL = 10

        TURNS = (GROUPS - 4) // 2

        def columns(g, width):
            return bass.ds(g.count(width, 0), width)

        def column(g, per_group, j):
            return bass.ds(g.count(per_group, j), 1)

        @block.sync
        def _(sp):
            def step(g):
                if g.plus(2).runs:
                    sp.wait_ge(x1_ready, g.count(1, 1))
                    sp.dma_start(x_in[g.parity][:], xT[:, columns(g.plus(2), N)]).then_inc(x_loaded[g.parity], 16)
                if not g.first:
                    sp.wait_ge(out_ready, g.count(1, 0))
                    sp.dma_start(v_in[:], fsT[:, columns(g, GB * R)]).then_inc(v_loaded, 16)
                    for half in range(2):
                        sp.dma_start(u_in[64 * half:64 * half + 64, :],
                                     fsR[columns(g, GB * R), :]).then_inc(u_loaded, 16)
                    sp.dma_start(outT[:, columns(g.plus(-1), N)], out_sb[:]).then_inc(out_stored, 16)

            sp.dma_start(x_in[0][:], xT[:, 0:N]).then_inc(x_loaded[0], 16)
            for n, w in enumerate((wfT, wiT, whT)):
                sp.dma_start(w_raw[:, n, :], w).then_inc(w0_loaded, 16)
            sp.dma_start(x_in[1][:], xT[:, N:2 * N]).then_inc(x_loaded[1], 16)
            sp.dma_start(w_raw[:, W1:W3, :], s1T).then_inc(wup_loaded, 16)
            sp.dma_start(w_raw[:, W3:WR, :], s3T).then_inc(wup_loaded, 16)
            sp.dma_start(w_raw[:, WR:WL, :], r1T).then_inc(wup_loaded, 16)
            sp.dma_start(w_raw[:, WL, :], wlT).then_inc(wup_loaded, 16)
            sp.dma_start(v_in[:], fsT[:, 0:GB * R]).then_inc(v_loaded, 16)
            for half in range(2):
                sp.dma_start(u_in[64 * half:64 * half + 64, :], fsR[0:GB * R, :]).then_inc(u_loaded, 16)
            sp.dma_start(down[:, 0:SU, :], s2T).then_inc(down_loaded, 16)
            sp.dma_start(down[:, SU:SU + E, :], r2T).then_inc(down_loaded, 16)

            step(Step(0))
            with sp.Fori(0, TURNS) as turn:
                step(Step(1, turn))
                step(Step(2, turn))
            step(Step(GROUPS - 3))
            step(Step(GROUPS - 2))
            step(Step(GROUPS - 1))
            sp.wait_ge(out_ready, GROUPS)
            sp.dma_start(outT[:, (GROUPS - 1) * N:GROUPS * N], out_sb[:]).then_inc(out_stored, 16)
            sp.wait_ge(out_stored, 16 * (GROUPS + 1))

        @block.scalar
        def _(act):
            act.dma_start(biases[:, 0:1], bf).then_inc(small_loaded, 16)
            act.dma_start(biases[:, 1:2], bi).then_inc(small_loaded, 16)
            act.dma_start(biases[:, 2:3], bh).then_inc(small_loaded, 16)
            act.dma_start(cond[:], condT).then_inc(small_loaded, 16)
            act.dma_start(wr_raw[:], wrT).then_inc(small_loaded, 16)
            act.dma_start(route_bias[:], rbias.partition_broadcast(128)).then_inc(small_loaded, 16)
            act.dma_start(biases[:, 3:4], fcb).then_inc(small_loaded, 16)
            act.dma_start(tok_i[:], itok.partition_broadcast(128)).then_inc(small_loaded, 16)
            act.dma_start(index[:], c_index).then_inc(small_loaded, 16)
            act.dma_start(rank[:], c_rank).then_inc(small_loaded, 16)
            act.dma_start(eye_raw[:], c_eye).then_inc(consts_loaded, 16)
            act.dma_start(sel_raw[:], c_sel).then_inc(consts_loaded, 16)
            act.dma_start(block_mask[:], c_block).then_inc(consts_loaded, 16)

            def gates(g):
                if g.first:
                    act.wait_ge(small_loaded, 16 * SMALL)
                act.wait_ge(gates_mm, g.count(3, 1))
                nc.scalar.activation(forget[:], bank[0][:], ACT.Sigmoid, bias=biases[:, 0:1]).then_inc(forget_ready, 1)
                act.wait_ge(gates_mm, g.count(3, 2))
                if not g.first:
                    act.wait_ge(input_norm_ready, g.count(1, 0))
                nc.scalar.activation(inp[:], bank[1][:], ACT.Sigmoid, bias=biases[:, 1:2]).then_inc(inp_ready, 1)
                act.wait_ge(gates_mm, g.count(3, 3))
                if not g.first:
                    act.wait_ge(new_info_ready, g.count(1, 0))
                nc.scalar.activation(cand[:], bank[2][:], ACT.Identity, bias=biases[:, 2:3]).then_inc(cand_ready, 1)

            def logs(g):
                nc.scalar.preload_act_table_set("natural_log_exp_and_others")
                act.wait_ge(gate_sum_ready, g.count(1, 1))
                nc.scalar.activation(log_sum[:], gate_sum[:], ACT.Ln).then_inc(log_sum_ready, 1)
                act.wait_ge(log_sum_ready, g.count(1, 1))
                nc.scalar.activation(inv_sum[:], log_sum[:], ACT.Exp, scale=-1.0).then_inc(inv_sum_ready, 1)
                act.wait_ge(forget_norm_ready, g.count(1, 1))
                if g.first:
                    act.wait_ge(pads_ready, 4)
                nc.scalar.activation(log_ret[:].rearrange("p (b s) -> p b s", b=GB)[:, :, 1:PAD],
                                     forget_norm[:].rearrange("p (b s) -> p b s", b=GB),
                                     ACT.Ln, bias=eps_col[:, 0:1]).then_inc(log_ret_ready, 1)
                act.wait_ge(log_scale_ready, g.count(1, 1))
                nc.scalar.activation(scaling[:], log_scale[:], ACT.Exp).then_inc(scaling_ready, 1)
                nc.scalar.activation(retained[:].rearrange("p (b s) -> p b s", b=GB),
                                     log_cum[:].rearrange("p (b s) -> p b s", b=GB)[:, :, 1:PAD],
                                     ACT.Exp).then_inc(retained_ready, 1)

            def scores(g):
                nc.scalar.preload_act_table_set("sigmoid_and_others")
                act.wait_ge(logits_ready, g.count(1, 1))
                nc.scalar.activation(score[:], logits[:], ACT.Sigmoid).then_inc(score_ready, 1)

            def shared(g):
                nc.scalar.preload_act_table_set("silu_and_others")
                for s in range(SU):
                    act.wait_ge(shared_mm, g.count(SU, s + 1))
                    if s >= 2 or not g.first:
                        act.wait_ge(h_shared_ready, g.count(SU, s - 1))
                    nc.scalar.activation(silu[s % 2][:], PAIRS[s][0][:], ACT.Silu).then_inc(silu_ready, 1)

            def experts(g):
                for e in range(E):
                    act.wait_ge(expert_mm, g.count(E, e + 1))
                    if e >= 3:
                        act.wait_ge(h_gated_ready, g.count(E, e - 2))
                    elif e == 0 and not g.first:
                        act.wait_ge(h_gated_ready, g.count(E, 0))
                    nc.scalar.activation(gelu[e % 3][:], bank[e % 3][:], ACT.Gelu).then_inc(gelu_ready, 1)

            def linear(g):
                if g.runs:
                    if g.first:
                        act.wait_ge(setup_step, SETUP_STEPS)
                    act.wait_ge(linear_mm, g.count(1, 1))
                    if not g.first:
                        act.wait_ge(x3_ready, g.count(1, 0))
                    for j in range(GB):
                        last = nc.scalar.activation(act2[:, j * S:(j + 1) * S], LINEAR[:, j * S:(j + 1) * S], ACT.Gelu,
                                                    bias=bias2[:, column(g, GB, j)])
                    last.then_inc(act2_ready, 1)

            def step(g):
                nxt, prev = g.plus(1), g.plus(-1)
                scores(g)
                if nxt.runs:
                    gates(nxt)
                shared(g)
                if nxt.runs:
                    logs(nxt)
                nc.scalar.preload_act_table_set("gelu_and_others")
                if not g.first:
                    linear(prev)
                experts(g)

            gates(Step(0))
            logs(Step(0))
            step(Step(0))
            with act.Fori(0, TURNS) as turn:
                step(Step(1, turn))
                step(Step(2, turn))
            step(Step(GROUPS - 3))
            step(Step(GROUPS - 2))
            step(Step(GROUPS - 1))
            linear(Step(GROUPS - 1))

        @block.gpsimd
        def _(pool):
            nc.gpsimd.memset(ones[:], 1.0).then_inc(consts_ready, 1)
            nc.gpsimd.memset(out_sb[:], 0.0).then_inc(out_stored, 16)

            def split_x(g):
                pool.wait_ge(x_hi_ready, g.count(1, 1))
                nc.gpsimd.tensor_tensor(x_lo[:], x_in[g.parity][:], x_hi[:].bitcast(F32), ALU.subtract)\
                    .then_inc(x_lo_ready, 1)

            def norms(g):
                pool.wait_ge(inv_sum_ready, g.count(1, 1))
                pool.wait_ge(inp_ready, g.count(1, 1))
                nc.gpsimd.tensor_tensor(input_norm[:], inp[:], inv_sum[:], ALU.mult).then_inc(input_norm_ready, 1)
                pool.wait_ge(input_norm_ready, g.count(1, 1))
                pool.wait_ge(cand_ready, g.count(1, 1))
                nc.gpsimd.tensor_tensor(new_info[:], input_norm[:], cand[:], ALU.mult).then_inc(new_info_ready, 1)

            def tail(g):
                pool.wait_ge(scaling_ready, g.count(1, 1))
                pool.wait_ge(new_info_ready, g.count(1, 1))
                if g.first:
                    pool.wait_ge(pads_ready, 4)
                nc.gpsimd.tensor_tensor(scaled[:].rearrange("p (b s) -> p b s", b=GB)[:, :, 1:PAD],
                                        scaling[:].rearrange("p (b s) -> p b s", b=GB),
                                        new_info[:].rearrange("p (b s) -> p b s", b=GB), ALU.mult)\
                    .then_inc(scaled_ready, 1)
                pool.wait_ge(hidden_ready, g.count(1, 1))
                nc.gpsimd.tensor_tensor(x1[g.parity][:], hidden[:], x_in[g.parity][:], ALU.add).then_inc(x1_ready, 1)
                pool.wait_ge(x1_hi_ready, g.count(1, 1))
                nc.gpsimd.tensor_tensor(x1_lo[g.parity][:], x1[g.parity][:], x1_hi[g.parity][:].bitcast(F32),
                                        ALU.subtract).then_inc(x1_lo_ready, 1)

            def output(g):
                if g.runs:
                    pool.wait_ge(act2_ready, g.count(1, 1))
                    pool.wait_ge(x2_ready, g.count(1, 1))
                    nc.gpsimd.tensor_tensor(x3[:], x2[:], act2[:], ALU.add).then_inc(x3_ready, 1)
                    pool.wait_ge(x3_ready, g.count(1, 1))
                    pool.wait_ge(out_stored, g.count(16, 16))
                    if g.first:
                        pool.wait_ge(setup_step, SETUP_STEPS)
                    nc.gpsimd.tensor_tensor(out_sb[:].rearrange("p (b s) -> p b s", b=GB),
                                            x3[:].rearrange("p (b s) -> p b s", b=GB),
                                            gain[:, columns(g, GB)].unsqueeze(2).to_broadcast([128, GB, S]),
                                            ALU.mult).then_inc(out_ready, 1)

            def step(g):
                nxt, prev = g.plus(1), g.plus(-1)
                if nxt.runs:
                    norms(nxt)
                    tail(nxt)
                if g.plus(2).runs:
                    split_x(g.plus(2))
                if not g.first:
                    output(prev)

            split_x(Step(0))
            norms(Step(0))
            tail(Step(0))
            split_x(Step(1))
            step(Step(0))
            with pool.Fori(0, TURNS) as turn:
                step(Step(1, turn))
                step(Step(2, turn))
            step(Step(GROUPS - 3))
            step(Step(GROUPS - 2))
            step(Step(GROUPS - 1))
            output(Step(GROUPS - 1))

        @block.vector
        def _(dve):
            def split_x(g):
                dve.wait_ge(x_loaded[g.parity], 16 * (g.start // 2 + 1) if g.register is None
                            else g.register * 16 + 16 * (g.start // 2 + 1))
                if not g.first:
                    dve.wait_ge(gates_mm, g.plus(-1).count(3, 3))
                nc.vector.tensor_copy(x_hi[:], x_in[g.parity][:]).then_inc(x_hi_ready, 1)

            def seq(t):
                return t[:].rearrange("p (b s) -> p b s", b=GB)

            def gate_total(g):
                dve.wait_ge(forget_ready, g.count(1, 1))
                dve.wait_ge(inp_ready, g.count(1, 1))
                nc.vector.scalar_tensor_tensor(gate_sum[:], forget[:], EPS, inp[:], ALU.add, ALU.add)\
                    .then_inc(gate_sum_ready, 1)

            def retention(g):
                dve.wait_ge(inv_sum_ready, g.count(1, 1))
                nc.vector.tensor_tensor(forget_norm[:], forget[:], inv_sum[:], ALU.mult).then_inc(forget_norm_ready, 1)
                dve.wait_ge(log_ret_ready, g.count(1, 1))
                if g.first:
                    dve.wait_ge(pads_ready, 4)
                if not g.first:
                    dve.wait_ge(retained_ready, g.count(1, 0))
                nc.vector.tensor_tensor_scan(log_cum[:], scan_mask[:], log_ret[:], 0.0, ALU.mult, ALU.add)\
                    .then_inc(log_cum_ready, 1)
                dve.wait_ge(log_cum_ready, g.count(1, 1))
                nc.vector.tensor_tensor(seq(log_scale), seq(log_cum)[:, :, S:PAD].to_broadcast([128, GB, S]),
                                        seq(log_cum)[:, :, 0:S], ALU.subtract).then_inc(log_scale_ready, 1)

            def recurrence(g):
                dve.wait_ge(scaled_ready, g.count(1, 1))
                nc.vector.tensor_tensor_scan(scaled_cum[:], scan_mask[:], scaled[:], 0.0, ALU.mult, ALU.add)\
                    .then_inc(scaled_cum_ready, 1)
                dve.wait_ge(scaled_cum_ready, g.count(1, 1))
                dve.wait_ge(retained_ready, g.count(1, 1))
                if not g.first:
                    dve.wait_ge(x1_ready, g.count(1, 0))
                for j in range(GB):
                    last = nc.vector.scalar_tensor_tensor(
                        hidden[:, j * S:(j + 1) * S], retained[:, j * S:(j + 1) * S], cond[:, column(g, GB, j)],
                        scaled_cum[:, j * PAD + 1:(j + 1) * PAD], ALU.mult, ALU.add)
                last.then_inc(hidden_ready, 1)

            def split_x1(g):
                dve.wait_ge(x1_ready, g.count(1, 1))
                nc.vector.tensor_copy(x1_hi[g.parity][:], x1[g.parity][:]).then_inc(x1_hi_ready, 1)

            def route_logits(g):
                dve.wait_ge(route_mm, g.count(1, 1))
                if g.first:
                    dve.wait_ge(route_cond_ready, 1)
                nc.vector.tensor_tensor(logits[:], ROUTE[:, 0:GB * E], route_cond[:, columns(g, GB * E)], ALU.add)\
                    .then_inc(logits_ready, 1)

            tt = nc.vector.tensor_tensor
            sc = score[:].rearrange("p (b e) -> p b e", b=GB)

            def wide(t):
                return t[:].unsqueeze(2).to_broadcast([128, GB, E])

            def per_expert(t):
                return t[:].unsqueeze(1).to_broadcast([128, GB, E])

            def gate_link(g, done):
                def link(ins):
                    nonlocal done
                    ins.then_inc(gate_step, 1)
                    dve.wait_ge(gate_step, g.count(GATE_STEPS, done))
                    done += 1
                return link

            def choose(g, link, a, src):
                link(nc.vector.tensor_reduce(t1["max" + a][:], t8[src][:], AX.X, ALU.max))
                link(tt(t8["top" + a][:], t8[src][:], wide(t1["max" + a]), ALU.is_equal))
                link(tt(t8["ranked" + a][:], t8["top" + a][:], per_expert(rank), ALU.mult))
                link(nc.vector.tensor_reduce(t1["first" + a][:], t8["ranked" + a][:], AX.X, ALU.max))
                link(tt(t8["one" + a][:], t8["ranked" + a][:], wide(t1["first" + a]), ALU.is_equal))

            def choose_first(g):
                link = gate_link(g, 1)
                dve.wait_ge(score_ready, g.count(1, 1))
                if not g.first:
                    dve.wait_ge(gates_T_mm, g.count(1, 0))
                link(tt(t8["biased"][:], sc, per_expert(route_bias), ALU.add))
                choose(g, link, "1", "biased")

            def choose_second(g):
                link = gate_link(g, 7)
                link(nc.vector.scalar_tensor_tensor(t8["rest"][:], t8["one1"][:], -BIG, t8["biased"][:],
                                                    ALU.mult, ALU.add))
                choose(g, link, "2", "rest")

            def gates_of_chosen(g):
                link = gate_link(g, 13)
                link(tt(t8["chosen"][:], t8["one1"][:], t8["one2"][:], ALU.add))
                link(tt(t8["kept"][:], t8["chosen"][:], sc, ALU.mult))
                link(nc.vector.tensor_reduce(t1["denom"][:], t8["kept"][:], AX.X, ALU.add))
                link(nc.vector.tensor_scalar(t1["denom_eps"][:], t1["denom"][:], 1e-9, None, ALU.add))
                link(nc.vector.reciprocal(t1["inv_denom"][:], t1["denom_eps"][:]))
                link(nc.vector.tensor_scalar(t1["valid"][:], t1["denom"][:], 1e-9, None, ALU.is_gt))
                link(tt(t1["gain_valid"][:], t1["inv_denom"][:], t1["valid"][:], ALU.mult))
                link(nc.vector.tensor_scalar(t1["fallback"][:], t1["valid"][:], -0.5, 0.5, ALU.mult, ALU.add))
                link(tt(t8["gate_a"][:], t8["kept"][:], wide(t1["gain_valid"]), ALU.mult))
                link(tt(t8["even"][:], t8["chosen"][:], wide(t1["fallback"]), ALU.mult))
                link(tt(t8["gate"][:], t8["gate_a"][:], t8["even"][:], ALU.add))
                link(nc.vector.tensor_copy(gate_parts[:, :, 0:E], t8["gate"][:]))
                tt(gate_parts[:, :, E:2 * E], t8["gate"][:], gate_parts[:, :, 0:E].bitcast(F32), ALU.subtract)\
                    .then_inc(gate_parts_ready, 1)

            def gates_out(g):
                dve.wait_ge(gates_T_mm, g.count(1, 1))
                if not g.first:
                    dve.wait_ge(gate_mm, g.plus(-1).count(E, E))
                nc.vector.tensor_copy(gates_T[:], ROUTE[:]).then_inc(gates_T_ready, 1)

            def shared(g, s):
                dve.wait_ge(silu_ready, g.count(SU, s + 1))
                if s == 0 and not g.first:
                    dve.wait_ge(down_mm, g.plus(-1).count(E, E))
                nc.vector.scalar_tensor_tensor(h_shared[:, s, :], silu[s % 2][:], 1.0 / SHARED,
                                               PAIRS[s][1][:], ALU.mult, ALU.mult)\
                    .then_inc(h_shared_ready, 1)

            def expert(g, e):
                dve.wait_ge(gelu_ready, g.count(E, e + 1))
                dve.wait_ge(gate_mm, g.count(E, e + 1))
                if e >= 3:
                    dve.wait_ge(down_mm, g.count(E, e - 2))
                nc.vector.tensor_tensor(h_gated[e % 3][:], gelu[e % 3][:], GATE[e % 2][:], ALU.mult)\
                    .then_inc(h_gated_ready, 1)

            def residual2(g):
                dve.wait_ge(down_mm, g.count(E, E))
                if not g.first:
                    dve.wait_ge(x3_ready, g.count(1, 0))
                nc.vector.scalar_tensor_tensor(x2[:], ACC[:], 1.0 / 4, x1[g.parity][:], ALU.mult, ALU.add)\
                    .then_inc(x2_ready, 1)
                dve.wait_ge(x2_ready, g.count(1, 1))
                nc.vector.tensor_copy(x2_hi[:], x2[:]).then_inc(x2_hi_ready, 1)
                dve.wait_ge(x2_hi_ready, g.count(1, 1))
                nc.vector.tensor_tensor(x2_lo[:], x2[:], x2_hi[:].bitcast(F32), ALU.subtract).then_inc(x2_lo_ready, 1)

            def split_v(g):
                dve.wait_ge(v_loaded, g.count(16, 16))
                if not g.first:
                    dve.wait_ge(z1_mm, g.count(1, 0))
                nc.vector.tensor_copy(v_parts[:, 0, :], v_in[:]).then_inc(v_hi_ready, 1)
                dve.wait_ge(v_hi_ready, g.count(1, 1))
                nc.vector.tensor_tensor(v_parts[:, 1, :], v_in[:], v_parts[:, 0, :].bitcast(F32), ALU.subtract)\
                    .then_inc(v_lo_ready, 1)

            def mask_z1(g):
                if g.runs:
                    dve.wait_ge(z1_mm, g.count(1, 1))
                    nc.vector.tensor_tensor(z1[:], block_mask[:], LOWRANK[:], ALU.mult).then_inc(z1_ready, 1)

            setup = [0]

            def link(ins):
                setup[0] += 1
                ins.then_inc(setup_step, 1)
                dve.wait_ge(setup_step, setup[0])

            nc.vector.memset(eps_col[:], EPS).then_inc(pads_ready, 1)
            nc.vector.memset(log_ret[:], 0.0).then_inc(pads_ready, 1)
            nc.vector.memset(scaled[:], 0.0).then_inc(pads_ready, 1)
            link(nc.vector.memset(scan_mask[:], 1.0))
            nc.vector.memset(seq(scan_mask)[:, :, 0:1], 0.0).then_inc(pads_ready, 1)
            dve.wait_ge(w0_loaded, 48)
            nc.vector.tensor_copy(w_hi[:, 0:W1, :], w_raw[:, 0:W1, :]).then_inc(w0_split, 1)
            split_x(Step(0))
            dve.wait_ge(w0_split, 1)
            nc.vector.tensor_tensor(w_lo[:, 0:W1, :], w_raw[:, 0:W1, :], w_hi[:, 0:W1, :].bitcast(F32), ALU.subtract)\
                .then_inc(w0_split, 1)

            dve.wait_ge(small_loaded, 16 * SMALL)
            nc.vector.tensor_scalar(keep[:], cond[:], KEEP, None, ALU.is_lt).then_inc(keep_ready, 1)
            link(nc.vector.tensor_copy(tok_f[:], tok_i[:]))
            link(nc.vector.tensor_scalar(hit_a[:], tok_f[:], index[:, 0:1], None, ALU.is_equal))
            link(nc.vector.tensor_scalar(hit_b[:], tok_f[:], index[:, 1:2], None, ALU.is_equal))
            link(nc.vector.tensor_tensor(hit_a[:], hit_a[:], hit_b[:], ALU.add))
            link(nc.vector.tensor_scalar(bias2[:], cond[:], biases[:, 3:4], None, ALU.add))
            link(nc.vector.tensor_copy(wr_hi[:], wr_raw[:, 0, :]))
            link(nc.vector.tensor_tensor(wr_lo[:], wr_raw[:, 0, :], wr_hi[:].bitcast(F32), ALU.subtract))

            gate_total(Step(0))
            retention(Step(0))
            dve.wait_ge(wup_loaded, 64)
            for a, b in ((W1, WR), (WR, BLOCKS)):
                nc.vector.tensor_copy(w_hi[:, a:b, :], w_raw[:, a:b, :]).then_inc(wup_split, 1)
                dve.wait_ge(wup_split, 1 if a == W1 else 3)
                nc.vector.tensor_tensor(w_lo[:, a:b, :], w_raw[:, a:b, :], w_hi[:, a:b, :].bitcast(F32), ALU.subtract)\
                    .then_inc(wup_split, 1)
                if a == W1:
                    recurrence(Step(0))
                    split_x1(Step(0))
            dve.wait_ge(kept_counted, 1)
            link(nc.vector.tensor_scalar(all_zero[:], bank[6][:, 0:B], 0.0, None, ALU.is_equal))
            link(nc.vector.tensor_tensor(hit_b[:], all_zero[:], hit_a[:], ALU.mult))
            dve.wait_ge(cond_routed, 1)
            nc.vector.tensor_copy(route_cond[:], bank[7][:, 0:B * E]).then_inc(route_cond_ready, 1)
            nc.vector.tensor_tensor(gain[:], hit_b[:], keep[:], ALU.max).then_inc(keep_ready, 1)
            dve.wait_ge(keep_ready, 2)
            dve.wait_ge(route_cond_ready, 1)
            link(nc.vector.tensor_scalar(gain[:], gain[:], 1.0, None, ALU.add))
            assert setup[0] == SETUP_STEPS
            dve.wait_ge(consts_loaded, 48)
            dve.wait_ge(consts_ready, 1)
            nc.vector.tensor_copy(eye[:], eye_raw[:]).then_inc(consts_ready, 1)
            nc.vector.tensor_copy(sel[:], sel_raw[:]).then_inc(consts_ready, 1)
            nc.vector.memset(gate_parts[:].bitcast(F32), 0.0).then_inc(consts_ready, 1)
            dve.wait_ge(consts_ready, 4)
            split_x(Step(1))

            def step(g):
                nxt, prev = g.plus(1), g.plus(-1)
                route_logits(g)
                if not g.first:
                    split_v(prev)
                if nxt.runs:
                    gate_total(nxt)
                choose_first(g)
                choose_second(g)
                shared(g, 0)
                shared(g, 1)
                gates_of_chosen(g)
                shared(g, 2)
                shared(g, 3)
                gates_out(g)
                if not g.first:
                    mask_z1(prev)
                if nxt.runs:
                    retention(nxt)
                for e in range(E):
                    expert(g, e)
                    if e == 1 and nxt.runs:
                        recurrence(nxt)
                    if e == 3 and nxt.runs:
                        split_x1(nxt)
                    if e == 4 and g.plus(2).runs:
                        split_x(g.plus(2))
                residual2(g)

            step(Step(0))
            with dve.Fori(0, TURNS) as turn:
                step(Step(1, turn))
                step(Step(2, turn))
            step(Step(GROUPS - 3))
            step(Step(GROUPS - 2))
            step(Step(GROUPS - 1))
            split_v(Step(GROUPS - 1))
            mask_z1(Step(GROUPS - 1))

        @block.tensor
        def _(pe):
            def split_product(out, w, hi, lo, start=True, stop=True):
                nc.tensor.matmul(out, w_hi[:, w, :], hi, start=start, stop=False)
                nc.tensor.matmul(out, w_lo[:, w, :], hi, start=False, stop=False)
                return nc.tensor.matmul(out, w_hi[:, w, :], lo, start=False, stop=stop)

            def gates(g):
                if g.first:
                    pe.wait_ge(w0_split, 2)
                elif g.start == 1:
                    pe.wait_ge(cand_ready, 1)
                else:
                    pe.wait_ge(gelu_ready, g.plus(-2).count(E, E))
                pe.wait_ge(x_hi_ready, g.count(1, 1))
                pe.wait_ge(x_lo_ready, g.count(1, 1))
                for n in (WF, WI, WH):
                    split_product(bank[n][:], n, x_hi[:], x_lo[:]).then_inc(gates_mm, 1)

            def route(g):
                pe.wait_ge(x1_hi_ready, g.count(1, 1))
                pe.wait_ge(x1_lo_ready, g.count(1, 1))
                if g.first:
                    pe.wait_ge(route_cond_ready, 1)
                else:
                    pe.wait_ge(gates_T_ready, g.count(1, 0))
                for j in range(GB):
                    out = ROUTE[:, j * E:(j + 1) * E]
                    hi, lo = (t[g.parity][:, j * S:(j + 1) * S] for t in (x1_hi, x1_lo))
                    nc.tensor.matmul(out, hi, wr_hi[:], start=True, stop=False)
                    nc.tensor.matmul(out, hi, wr_lo[:], start=False, stop=False)
                    last = nc.tensor.matmul(out, lo, wr_hi[:], start=False, stop=True)
                last.then_inc(route_mm, 1)

            def shared(g):
                if g.first:
                    pe.wait_ge(wup_split, 4)
                for s in range(SU):
                    if s == 0 and not g.first:
                        pe.wait_ge(h_gated_ready, g.count(E, 0))
                    elif s == 1 and not g.first:
                        pe.wait_ge(x2_ready, g.count(1, 0))
                    elif s == 2:
                        if g.plus(1).runs:
                            pe.wait_ge(cand_ready, g.plus(1).count(1, 1))
                        else:
                            pe.wait_ge(gelu_ready, g.count(E, 0))
                    elif s == 3:
                        pe.wait_ge(silu_ready, g.count(SU, 1))
                    hi, lo = x1_hi[g.parity][:], x1_lo[g.parity][:]
                    split_product(PAIRS[s][0][:], W1 + s, hi, lo)
                    split_product(PAIRS[s][1][:], W3 + s, hi, lo).then_inc(shared_mm, 1)

            def transpose_gates(g):
                pe.wait_ge(gate_parts_ready, g.count(1, 1))
                if g.first:
                    pe.wait_ge(consts_ready, 4)
                for j in range(GB):
                    last = nc.tensor.matmul(ROUTE[:, j * S:(j + 1) * S], gate_parts[:, j, :], eye[:],
                                            start=True, stop=True)
                last.then_inc(gates_T_mm, 1)

            def low_rank(g):
                if g.runs:
                    pe.wait_ge(x2_lo_ready, g.count(1, 1))
                    pe.wait_ge(v_lo_ready, g.count(1, 1))
                    if g.plus(1).runs:
                        pe.wait_ge(silu_ready, g.plus(1).count(SU, 2))
                    v = v_parts[:].rearrange("p h k -> p (h k)")
                    nc.tensor.matmul(LOWRANK[:], v, x2_hi[:], start=True, stop=False)
                    nc.tensor.matmul(LOWRANK[:], v, x2_lo[:], start=False, stop=True).then_inc(z1_mm, 1)

            def linear(g):
                if g.runs:
                    if g.plus(1).runs:
                        pe.wait_ge(h_shared_ready, g.plus(1).count(SU, 1))
                    split_product(LINEAR[:], WL, x2_hi[:], x2_lo[:], stop=False)
                    pe.wait_ge(z1_ready, g.count(1, 1))
                    pe.wait_ge(u_loaded, g.count(32, 32))
                    nc.tensor.matmul(LINEAR[:], u_in[:], z1[:], start=False, stop=True).then_inc(linear_mm, 1)

            def up(g, e):
                if e < 3:
                    if e == 0:
                        pe.wait_ge(h_shared_ready, g.count(SU, SU))
                else:
                    pe.wait_ge(gelu_ready, g.count(E, e - 2))
                split_product(bank[e % 3][:], WR + e, x1_hi[g.parity][:], x1_lo[g.parity][:]).then_inc(expert_mm, 1)

            def spread_gate(g, e):
                if e == 0:
                    pe.wait_ge(gates_T_ready, g.count(1, 1))
                if e == 1 and not g.first:
                    pe.wait_ge(act2_ready, g.count(1, 0))
                if e >= 2:
                    pe.wait_ge(h_gated_ready, g.count(E, e - 1))
                nc.tensor.matmul(GATE[e % 2][:], sel[:, e, :], gates_T[:], start=True, stop=True).then_inc(gate_mm, 1)

            def shared_down(g):
                if g.first:
                    pe.wait_ge(down_loaded, 32)
                else:
                    pe.wait_ge(x2_ready, g.count(1, 0))
                pe.wait_ge(h_shared_ready, g.count(SU, SU))
                for s in range(SU):
                    nc.tensor.matmul(ACC[:], down[:, s, :], h_shared[:, s, :], start=(s == 0), stop=False)

            def expert_down(g, e):
                pe.wait_ge(h_gated_ready, g.count(E, e + 1))
                nc.tensor.matmul(ACC[:], down[:, SU + e, :], h_gated[e % 3][:], start=False, stop=(e == E - 1))\
                    .then_inc(down_mm, 1)

            def step(g):
                nxt, prev = g.plus(1), g.plus(-1)
                route(g)
                if nxt.runs:
                    gates(nxt)
                shared(g)
                if not g.first:
                    low_rank(prev)
                transpose_gates(g)
                shared_down(g)
                if not g.first:
                    linear(prev)
                up(g, 0)
                up(g, 1)
                spread_gate(g, 0)
                for e in range(E):
                    if e + 2 < E:
                        up(g, e + 2)
                    if e + 1 < E:
                        spread_gate(g, e + 1)
                    expert_down(g, e)

            gates(Step(0))
            pe.wait_ge(keep_ready, 1)
            pe.wait_ge(consts_ready, 1)
            nc.tensor.matmul(bank[6][:, 0:B], ones[:], keep[:], start=True, stop=True).then_inc(kept_counted, 1)
            for b in range(B):
                last = nc.tensor.matmul(bank[7][:, b * E:(b + 1) * E], cond[:, b:b + 1].to_broadcast([128, 128]),
                                        wr_raw[:, 1, :], start=True, stop=True)
            last.then_inc(cond_routed, 1)
            step(Step(0))
            with pe.Fori(0, TURNS) as turn:
                step(Step(1, turn))
                step(Step(2, turn))
            step(Step(GROUPS - 3))
            step(Step(GROUPS - 2))
            step(Step(GROUPS - 1))
            low_rank(Step(GROUPS - 1))
            linear(Step(GROUPS - 1))


_OUT = (D, B * S)


def kernel(x, cond_1024, fside_Bx1x1024x16_0, itok_B_14_1018, L0_cond_W_f, L0_cond_b_f, L0_cond_W_i, L0_cond_b_i,
           L0_cond_W_h, L0_cond_b_h, L1_cond_W_router, L1_cond_router_bias, L1_cond_s_w1, L1_cond_s_w3, L1_cond_s_w2,
           L1_cond_r_w1, L1_cond_r_w2, L2_cond_W, L2_cond_fc_bias):
    import numpy as np
    import concourse.bacc as bacc
    from concourse.bass_utils import run_bass_kernel_spmd

    def lay(a, *axes):
        a = np.asarray(a)
        return np.ascontiguousarray(a.transpose(*axes) if axes else a)

    fside = np.asarray(fside_Bx1x1024x16_0)
    s_w1, s_w3, s_w2 = (np.asarray(a) for a in (L1_cond_s_w1, L1_cond_s_w3, L1_cond_s_w2))
    f = np.float32
    k = np.arange(128)
    sequence = (k % (GB * R)) // R
    block_mask = np.where(sequence[:, None] == np.arange(N)[None, :] // S, f(1.0 / (D * R)), f(0)).astype(f)
    sel = np.zeros((128, E, 128), f)
    for e in range(E):
        sel[e, e, :] = 1
        sel[E + e, e, :] = 1
    arrays = {
        "xT": lay(np.asarray(x).reshape(B * S, D), 1, 0),
        "condT": lay(cond_1024, 1, 0),
        "fsT": lay(fside[:, 0], 1, 0, 2).reshape(D, B * R),
        "fsR": lay(fside[:, 0], 0, 2, 1).reshape(B * R, D),
        "itok": lay(itok_B_14_1018),
        "wfT": lay(L0_cond_W_f, 1, 0), "bf": lay(L0_cond_b_f).reshape(D, 1),
        "wiT": lay(L0_cond_W_i, 1, 0), "bi": lay(L0_cond_b_i).reshape(D, 1),
        "whT": lay(L0_cond_W_h, 1, 0), "bh": lay(L0_cond_b_h).reshape(D, 1),
        "wrT": lay(np.asarray(L1_cond_W_router).reshape(E, 2, D), 2, 1, 0),
        "rbias": lay(L1_cond_router_bias),
        "s1T": lay(s_w1.reshape(SU, 128, D), 2, 0, 1),
        "s3T": lay(s_w3.reshape(SU, 128, D), 2, 0, 1),
        "s2T": lay(s_w2.reshape(SHARED, D, 2, 128), 3, 0, 2, 1).reshape(128, SU, D),
        "r1T": lay(L1_cond_r_w1, 2, 0, 1),
        "r2T": lay(L1_cond_r_w2, 2, 0, 1),
        "wlT": lay(L2_cond_W, 1, 0), "fcb": lay(L2_cond_fc_bias).reshape(D, 1),
        "c_block": block_mask,
        "c_sel": sel,
        "c_eye": np.eye(128, dtype=f),
        "c_index": np.stack([k, k - D], 1).astype(f),
        "c_rank": np.ascontiguousarray(np.broadcast_to((E - np.arange(E)).astype(f), (128, E))),
    }
    nc = bacc.Bacc("TRN2", target_bir_lowering=False, num_devices=1)
    args = [nc.dram_tensor(f"in_{n}", a.shape, mybir.dt.from_np(a.dtype), kind="ExternalInput").ap()
            for n, a in arrays.items()]
    out = nc.dram_tensor("out_T", _OUT, mybir.dt.float32, kind="ExternalOutput").ap()
    build(nc, *args, out)
    r = run_bass_kernel_spmd(nc, [{f"in_{n}": a for n, a in arrays.items()}], core_ids=[0])
    outT = r.results[0]["out_T"]
    return np.ascontiguousarray(np.asarray(outT).reshape(D, B, S).transpose(1, 2, 0))
```

```python
import concourse.bass as bass
from concourse import mybir
from contextlib import ExitStack

B, S, D = 32, 128, 128
R = 16
E = 8
SHARED = 2
GB = 4
N = GB * S
GROUPS = B // GB
PAD = S + 1
EPS = 1e-8
KEEP = 0.8
BIG = 3.0e38
SU = SHARED * 2
WF, WI, WH = 0, 1, 2
W1, W3 = 3, 3 + SU
WR = 3 + 2 * SU
WL = WR + E
BLOCKS = WL + 1


class Step:

    def __init__(self, start, register=None, step=2):
        self.start, self.register, self.step = start, register, step

    def plus(self, n):
        return Step(self.start + n, self.register, self.step)

    @property
    def runs(self):
        return self.register is not None or 0 <= self.start < GROUPS

    @property
    def first(self):
        return self.register is None and self.start == 0

    @property
    def parity(self):
        return self.start % 2

    def count(self, per_group, k):
        if self.register is None:
            return self.start * per_group + k
        return self.register * (self.step * per_group) + (self.start * per_group + k)


COND, BIASES, ROUTER, ROUTE_BIAS, INDEX, RANK = 0, B, B + 4, B + 4 + 2 * E, B + 4 + 3 * E, B + 6 + 3 * E
SMALL = RANK + E


def build(nc, xT, small_in, fsT, fsR, itok, gatesT, s1T, s3T, s2T, r1T, r2T, wlT, c_block, c_sel, c_eye, outT):
    F32, F32R, I32 = mybir.dt.float32, mybir.dt.float32r, mybir.dt.int32
    ALU, ACT, AX = mybir.AluOpType, mybir.ActivationFunctionType, mybir.AxisListType

    with ExitStack() as ctx:
        def sb(name, shape, dt=F32):
            return ctx.enter_context(nc.sbuf_tensor(name, shape, dt))

        def sem(name):
            return ctx.enter_context(nc.semaphore(name))

        w_raw = sb("w_raw", [128, BLOCKS, 128])
        w_hi = sb("w_hi", [128, BLOCKS, 128], F32R)
        w_lo = sb("w_lo", [128, BLOCKS, 128], F32R)
        down = sb("down", [128, SU + E, 128])
        small = sb("small", [128, SMALL])
        wr_raw = small[:, ROUTER:ROUTER + 2 * E].rearrange("p (h e) -> p h e", h=2)
        wr_hi = sb("wr_hi", [128, E], F32R)
        wr_lo = sb("wr_lo", [128, E], F32R)
        cond = small[:, COND:COND + B]
        biases = small[:, BIASES:BIASES + 4]
        route_bias = small[:, ROUTE_BIAS:ROUTE_BIAS + E]
        rank = small[:, RANK:RANK + E]
        index = small[:, INDEX:INDEX + 2]
        cond_weight = sb("cond_weight", [128, B, E])
        block_mask = sb("block_mask", [128, N])
        sel_raw = sb("sel_raw", [128, E, 128])
        sel = sb("sel", [128, E, 128], F32R)
        eye_raw = sb("eye_raw", [128, 128])
        eye = sb("eye", [128, 128], F32R)
        eps_col = sb("eps_col", [128, 1])
        ones = sb("ones", [128, 128])
        scan_mask = sb("scan_mask", [128, GB * PAD])
        tok_i = sb("tok_i", [128, B], I32)
        tok_f = sb("tok_f", [128, B])
        keep = sb("keep", [128, B])
        all_zero = sb("all_zero", [128, B])
        hit_a = sb("hit_a", [128, B])
        hit_b = sb("hit_b", [128, B])
        gain = sb("gain", [128, B])
        bias2 = sb("bias2", [128, B])
        route_cond = sb("route_cond", [128, B * E])

        x_in = sb("x_in", [128, N])
        x_res = sb("x_res", [128, N])
        x_hi = sb("x_hi", [128, N], F32R)
        x_lo = sb("x_lo", [128, N], F32R)
        forget = sb("forget", [128, N])
        inp = sb("inp", [128, N])
        cand = sb("cand", [128, N])
        gate_sum = sb("gate_sum", [128, N])
        log_sum = sb("log_sum", [128, N])
        inv_sum = sb("inv_sum", [128, N])
        forget_norm = sb("forget_norm", [128, N])
        input_norm = sb("input_norm", [128, N])
        new_info = sb("new_info", [128, N])
        log_ret = sb("log_ret", [128, GB * PAD])
        log_cum = sb("log_cum", [128, GB * PAD])
        log_scale = sb("log_scale", [128, N])
        scaling = sb("scaling", [128, N])
        retained = sb("retained", [128, N])
        scaled = sb("scaled", [128, GB * PAD])
        scaled_cum = sb("scaled_cum", [128, GB * PAD])
        hidden = sb("hidden", [128, N])
        x1 = [sb(f"x1_{p}", [128, N]) for p in range(2)]
        x1_hi = [sb(f"x1_hi{p}", [128, N], F32R) for p in range(2)]
        x1_lo = [sb(f"x1_lo{p}", [128, N], F32R) for p in range(2)]

        logits = sb("logits", [128, GB * E])
        score = sb("score", [128, GB * E])
        t8 = {n: sb(n, [128, GB, E]) for n in
              ("biased", "top1", "ranked1", "one1", "rest", "top2", "ranked2", "one2", "chosen", "kept", "even",
               "gate_a", "gate")}
        t1 = {n: sb(n, [128, GB]) for n in
              ("max1", "first1", "max2", "first2", "denom", "denom_eps", "inv_denom", "valid", "gain_valid",
               "fallback")}
        gate_parts = sb("gate_parts", [128, GB, 128], F32R)
        gates_T = sb("gates_T", [128, N], F32R)
        silu = [sb(f"silu{p}", [128, N]) for p in range(2)]
        h_shared = sb("h_shared", [128, SU, N])
        gelu = [sb(f"gelu{p}", [128, N]) for p in range(3)]
        h_gated = [sb(f"h_gated{p}", [128, N]) for p in range(3)]
        x2 = sb("x2", [128, N])
        x2_hi = sb("x2_hi", [128, N], F32R)
        x2_lo = sb("x2_lo", [128, N], F32R)

        v_in = sb("v_in", [128, GB * R])
        v_parts = sb("v_parts", [128, 2, GB * R], F32R)
        u_in = sb("u_in", [128, 128])
        z1 = sb("z1", [128, N])
        act2 = sb("act2", [128, N])
        x3 = sb("x3", [128, N])
        out_sb = sb("out_sb", [128, N])

        bank = [ctx.enter_context(nc.psum_tensor(f"bank{i}", [128, N], F32)) for i in range(8)]
        ACC, ROUTE, LOWRANK, LINEAR = bank[5], bank[6], bank[7], bank[4]
        GATE = (bank[3], bank[7])
        PAIRS = ((bank[3], bank[4]), (bank[7], bank[5]), (bank[0], bank[1]), (bank[2], bank[3]))

        w0_loaded, wup_loaded, down_loaded = sem("w0_loaded"), sem("wup_loaded"), sem("down_loaded")
        small_loaded, consts_loaded = sem("small_loaded"), sem("consts_loaded")
        x_loaded, x_res_loaded = sem("x_loaded"), sem("x_res_loaded")
        v_loaded, u_loaded, out_stored = sem("v_loaded"), sem("u_loaded"), sem("out_stored")
        w0_split, wup_split, consts_ready = sem("w0_split"), sem("wup_split"), sem("consts_ready")
        pads_ready, keep_ready, kept_counted = sem("pads_ready"), sem("keep_ready"), sem("kept_counted")
        setup_step, cond_routed, route_cond_ready = sem("setup_step"), sem("cond_routed"), sem("route_cond_ready")
        x_hi_ready, x_lo_ready, gates_mm = sem("x_hi_ready"), sem("x_lo_ready"), sem("gates_mm")
        forget_ready, inp_ready, cand_ready = sem("forget_ready"), sem("inp_ready"), sem("cand_ready")
        gate_sum_ready, log_sum_ready, inv_sum_ready = sem("gate_sum_ready"), sem("log_sum_ready"), sem("inv_sum_ready")
        forget_norm_ready, input_norm_ready = sem("forget_norm_ready"), sem("input_norm_ready")
        new_info_ready, log_ret_ready, log_cum_ready = sem("new_info_ready"), sem("log_ret_ready"), sem("log_cum_ready")
        log_scale_ready, scaling_ready, retained_ready = sem("log_scale_ready"), sem("scaling_ready"), sem("retained_ready")
        scaled_ready, scaled_cum_ready, hidden_ready = sem("scaled_ready"), sem("scaled_cum_ready"), sem("hidden_ready")
        x1_ready, x1_hi_ready, x1_lo_ready = sem("x1_ready"), sem("x1_hi_ready"), sem("x1_lo_ready")
        route_mm, logits_ready, score_ready = sem("route_mm"), sem("logits_ready"), sem("score_ready")
        gate_step, gate_parts_ready = sem("gate_step"), sem("gate_parts_ready")
        gates_T_mm, gates_T_ready = sem("gates_T_mm"), sem("gates_T_ready")
        shared_mm, silu_ready, h_shared_ready = sem("shared_mm"), sem("silu_ready"), sem("h_shared_ready")
        expert_mm, gate_mm, gelu_ready = sem("expert_mm"), sem("gate_mm"), sem("gelu_ready")
        h_gated_ready, down_mm = sem("h_gated_ready"), sem("down_mm")
        x2_ready, x2_hi_ready, x2_lo_ready = sem("x2_ready"), sem("x2_hi_ready"), sem("x2_lo_ready")
        v_hi_ready, v_lo_ready = sem("v_hi_ready"), sem("v_lo_ready")
        z1_mm, z1_ready, linear_mm, act2_ready = sem("z1_mm"), sem("z1_ready"), sem("linear_mm"), sem("act2_ready")
        x3_ready, out_ready = sem("x3_ready"), sem("out_ready")

        block = ctx.enter_context(nc.Block())

        GATE_STEPS = 24
        SETUP_STEPS = 11

        TURNS = (GROUPS - 4) // 2

        def columns(g, width):
            return bass.ds(g.count(width, 0), width)

        def column(g, per_group, j):
            return bass.ds(g.count(per_group, j), 1)

        @block.sync
        def _(sp):
            def step(g):
                if g.plus(3).runs:
                    sp.wait_ge(x_lo_ready, g.plus(2).count(1, 1))
                    sp.dma_start(x_in[:], xT[:, columns(g.plus(3), N)]).then_inc(x_loaded, 16)
                if g.plus(2).runs:
                    sp.wait_ge(x1_ready, g.plus(1).count(1, 1))
                    sp.dma_start(x_res[:], xT[:, columns(g.plus(2), N)]).then_inc(x_res_loaded, 16)
                if not g.first:
                    sp.wait_ge(out_ready, g.count(1, 0))
                    sp.dma_start(v_in[:], fsT[:, columns(g, GB * R)]).then_inc(v_loaded, 16)
                    for half in range(2):
                        sp.dma_start(u_in[64 * half:64 * half + 64, :],
                                     fsR[columns(g, GB * R), :]).then_inc(u_loaded, 16)
                    sp.dma_start(outT[:, columns(g.plus(-1), N)], out_sb[:]).then_inc(out_stored, 16)

            sp.dma_start(x_in[:], xT[:, 0:N]).then_inc(x_loaded, 16)
            sp.dma_start(w_raw[:, 0:W1, :], gatesT).then_inc(w0_loaded, 16)
            sp.dma_start(x_res[:], xT[:, 0:N]).then_inc(x_res_loaded, 16)
            sp.dma_start(w_raw[:, W1:W3, :], s1T).then_inc(wup_loaded, 16)
            sp.dma_start(w_raw[:, W3:WR, :], s3T).then_inc(wup_loaded, 16)
            sp.dma_start(w_raw[:, WR:WL, :], r1T).then_inc(wup_loaded, 16)
            sp.dma_start(w_raw[:, WL, :], wlT).then_inc(wup_loaded, 16)
            sp.dma_start(v_in[:], fsT[:, 0:GB * R]).then_inc(v_loaded, 16)
            for half in range(2):
                sp.dma_start(u_in[64 * half:64 * half + 64, :], fsR[0:GB * R, :]).then_inc(u_loaded, 16)
            sp.dma_start(down[:, 0:SU, :], s2T).then_inc(down_loaded, 16)
            sp.dma_start(down[:, SU:SU + E, :], r2T).then_inc(down_loaded, 16)

            sp.wait_ge(x_lo_ready, 1)
            sp.dma_start(x_in[:], xT[:, N:2 * N]).then_inc(x_loaded, 16)
            sp.wait_ge(x1_ready, 1)
            sp.dma_start(x_res[:], xT[:, N:2 * N]).then_inc(x_res_loaded, 16)
            sp.wait_ge(x_lo_ready, 2)
            sp.dma_start(x_in[:], xT[:, 2 * N:3 * N]).then_inc(x_loaded, 16)
            step(Step(0))
            with sp.Fori(0, TURNS) as turn:
                step(Step(1, turn))
                step(Step(2, turn))
            step(Step(GROUPS - 3))
            step(Step(GROUPS - 2))
            step(Step(GROUPS - 1))
            sp.wait_ge(out_ready, GROUPS)
            sp.dma_start(outT[:, (GROUPS - 1) * N:GROUPS * N], out_sb[:]).then_inc(out_stored, 16)
            sp.wait_ge(out_stored, 16 * (GROUPS + 1))

        @block.scalar
        def _(act):
            nc.scalar.preload_act_table_set("sigmoid_and_others")
            act.dma_start(small[:], small_in).then_inc(small_loaded, 16)
            act.dma_start(tok_i[:], itok.partition_broadcast(128)).then_inc(small_loaded, 16)
            act.dma_start(eye_raw[:], c_eye).then_inc(consts_loaded, 16)
            act.dma_start(sel_raw[:], c_sel).then_inc(consts_loaded, 16)
            act.dma_start(block_mask[:], c_block).then_inc(consts_loaded, 16)

            def gates(g):
                if g.first:
                    act.wait_ge(small_loaded, 32)
                act.wait_ge(gates_mm, g.count(3, 1))
                nc.scalar.activation(forget[:], bank[0][:], ACT.Sigmoid, bias=biases[:, 0:1]).then_inc(forget_ready, 1)
                act.wait_ge(gates_mm, g.count(3, 2))
                if not g.first:
                    act.wait_ge(input_norm_ready, g.count(1, 0))
                nc.scalar.activation(inp[:], bank[1][:], ACT.Sigmoid, bias=biases[:, 1:2]).then_inc(inp_ready, 1)
                act.wait_ge(gates_mm, g.count(3, 3))
                if not g.first:
                    act.wait_ge(new_info_ready, g.count(1, 0))
                nc.scalar.activation(cand[:], bank[2][:], ACT.Identity, bias=biases[:, 2:3]).then_inc(cand_ready, 1)

            def logs(g, before):
                nc.scalar.preload_act_table_set("natural_log_exp_and_others")
                if g.runs:
                    act.wait_ge(gate_sum_ready, g.count(1, 1))
                    nc.scalar.activation(log_sum[:], gate_sum[:], ACT.Ln).then_inc(log_sum_ready, 1)
                    act.wait_ge(log_sum_ready, g.count(1, 1))
                    nc.scalar.activation(inv_sum[:], log_sum[:], ACT.Exp, scale=-1.0).then_inc(inv_sum_ready, 1)
                if before.runs:
                    act.wait_ge(log_scale_ready, before.count(1, 1))
                    nc.scalar.activation(scaling[:], log_scale[:], ACT.Exp).then_inc(scaling_ready, 1)
                    nc.scalar.activation(retained[:].rearrange("p (b s) -> p b s", b=GB),
                                         log_cum[:].rearrange("p (b s) -> p b s", b=GB)[:, :, 1:PAD],
                                         ACT.Exp).then_inc(retained_ready, 1)
                if g.runs:
                    act.wait_ge(forget_norm_ready, g.count(1, 1))
                    if g.first:
                        act.wait_ge(pads_ready, 4)
                    nc.scalar.activation(log_ret[:].rearrange("p (b s) -> p b s", b=GB)[:, :, 1:PAD],
                                         forget_norm[:].rearrange("p (b s) -> p b s", b=GB),
                                         ACT.Ln, bias=eps_col[:, 0:1]).then_inc(log_ret_ready, 1)

            def scores(g):
                nc.scalar.preload_act_table_set("sigmoid_and_others")
                act.wait_ge(logits_ready, g.count(1, 1))
                nc.scalar.activation(score[:], logits[:], ACT.Sigmoid).then_inc(score_ready, 1)

            def shared(g):
                nc.scalar.preload_act_table_set("silu_and_others")
                for s in range(SU):
                    act.wait_ge(shared_mm, g.count(SU, s + 1))
                    if s >= 2 or not g.first:
                        act.wait_ge(h_shared_ready, g.count(SU, s - 1))
                    nc.scalar.activation(silu[s % 2][:], PAIRS[s][0][:], ACT.Silu).then_inc(silu_ready, 1)

            def experts(g, prev):
                for e in range(E):
                    if e == 3:
                        linear(prev)
                    act.wait_ge(expert_mm, g.count(E, e + 1))
                    if e >= 3:
                        act.wait_ge(h_gated_ready, g.count(E, e - 2))
                    elif e == 0 and not g.first:
                        act.wait_ge(h_gated_ready, g.count(E, 0))
                    nc.scalar.activation(gelu[e % 3][:], bank[e % 3][:], ACT.Gelu).then_inc(gelu_ready, 1)

            def linear(g):
                if g.runs:
                    if g.first:
                        act.wait_ge(setup_step, SETUP_STEPS)
                    act.wait_ge(linear_mm, g.count(1, 1))
                    if not g.first:
                        act.wait_ge(x3_ready, g.count(1, 0))
                    for j in range(GB):
                        last = nc.scalar.activation(act2[:, j * S:(j + 1) * S], LINEAR[:, j * S:(j + 1) * S], ACT.Gelu,
                                                    bias=bias2[:, column(g, GB, j)])
                    last.then_inc(act2_ready, 1)

            def step(g):
                scores(g)
                if g.plus(2).runs:
                    gates(g.plus(2))
                shared(g)
                if g.plus(1).runs:
                    logs(g.plus(2), g.plus(1))
                nc.scalar.preload_act_table_set("gelu_and_others")
                experts(g, g.plus(-1))

            gates(Step(0))
            logs(Step(0), Step(-1))
            logs(Step(-1), Step(0))
            nc.scalar.preload_act_table_set("sigmoid_and_others")
            gates(Step(1))
            logs(Step(1), Step(-1))
            step(Step(0))
            with act.Fori(0, TURNS) as turn:
                step(Step(1, turn))
                step(Step(2, turn))
            step(Step(GROUPS - 3))
            step(Step(GROUPS - 2))
            step(Step(GROUPS - 1))
            linear(Step(GROUPS - 1))

        @block.gpsimd
        def _(pool):
            nc.gpsimd.memset(ones[:], 1.0).then_inc(consts_ready, 1)
            nc.gpsimd.memset(out_sb[:], 0.0).then_inc(out_stored, 16)

            def split_x(g):
                pool.wait_ge(x_hi_ready, g.count(1, 1))
                nc.gpsimd.tensor_tensor(x_lo[:], x_in[:], x_hi[:].bitcast(F32), ALU.subtract)\
                    .then_inc(x_lo_ready, 1)

            def input_norms(g):
                pool.wait_ge(inv_sum_ready, g.count(1, 1))
                pool.wait_ge(inp_ready, g.count(1, 1))
                nc.gpsimd.tensor_tensor(input_norm[:], inp[:], inv_sum[:], ALU.mult).then_inc(input_norm_ready, 1)

            def new_infos(g):
                pool.wait_ge(input_norm_ready, g.count(1, 1))
                pool.wait_ge(cand_ready, g.count(1, 1))
                if not g.first:
                    pool.wait_ge(scaled_ready, g.count(1, 0))
                nc.gpsimd.tensor_tensor(new_info[:], input_norm[:], cand[:], ALU.mult).then_inc(new_info_ready, 1)

            def scale(g):
                pool.wait_ge(scaling_ready, g.count(1, 1))
                pool.wait_ge(new_info_ready, g.count(1, 1))
                if g.first:
                    pool.wait_ge(pads_ready, 4)
                nc.gpsimd.tensor_tensor(scaled[:].rearrange("p (b s) -> p b s", b=GB)[:, :, 1:PAD],
                                        scaling[:].rearrange("p (b s) -> p b s", b=GB),
                                        new_info[:].rearrange("p (b s) -> p b s", b=GB), ALU.mult)\
                    .then_inc(scaled_ready, 1)

            def residual1(g):
                pool.wait_ge(hidden_ready, g.count(1, 1))
                pool.wait_ge(x_res_loaded, g.count(16, 16))
                nc.gpsimd.tensor_tensor(x1[g.parity][:], hidden[:], x_res[:], ALU.add).then_inc(x1_ready, 1)
                pool.wait_ge(x1_hi_ready, g.count(1, 1))
                nc.gpsimd.tensor_tensor(x1_lo[g.parity][:], x1[g.parity][:], x1_hi[g.parity][:].bitcast(F32),
                                        ALU.subtract).then_inc(x1_lo_ready, 1)

            def output(g):
                if g.runs:
                    pool.wait_ge(act2_ready, g.count(1, 1))
                    pool.wait_ge(x2_ready, g.count(1, 1))
                    nc.gpsimd.tensor_tensor(x3[:], x2[:], act2[:], ALU.add).then_inc(x3_ready, 1)
                    pool.wait_ge(x3_ready, g.count(1, 1))
                    pool.wait_ge(out_stored, g.count(16, 16))
                    if g.first:
                        pool.wait_ge(setup_step, SETUP_STEPS)
                    nc.gpsimd.tensor_tensor(out_sb[:].rearrange("p (b s) -> p b s", b=GB),
                                            x3[:].rearrange("p (b s) -> p b s", b=GB),
                                            gain[:, columns(g, GB)].unsqueeze(2).to_broadcast([128, GB, S]),
                                            ALU.mult).then_inc(out_ready, 1)

            def step(g):
                nxt, after_next = g.plus(1), g.plus(2)
                if after_next.runs:
                    input_norms(after_next)
                if nxt.runs:
                    scale(nxt)
                if after_next.runs:
                    new_infos(after_next)
                if nxt.runs:
                    residual1(nxt)
                if g.plus(3).runs:
                    split_x(g.plus(3))
                if not g.first:
                    output(g.plus(-1))

            split_x(Step(0))
            split_x(Step(1))
            input_norms(Step(0))
            new_infos(Step(0))
            scale(Step(0))
            residual1(Step(0))
            split_x(Step(2))
            input_norms(Step(1))
            new_infos(Step(1))
            step(Step(0))
            with pool.Fori(0, TURNS) as turn:
                step(Step(1, turn))
                step(Step(2, turn))
            step(Step(GROUPS - 3))
            step(Step(GROUPS - 2))
            step(Step(GROUPS - 1))
            output(Step(GROUPS - 1))

        @block.vector
        def _(dve):
            def split_x(g):
                dve.wait_ge(x_loaded, g.count(16, 16))
                if not g.first:
                    dve.wait_ge(gates_mm, g.plus(-1).count(3, 3))
                nc.vector.tensor_copy(x_hi[:], x_in[:]).then_inc(x_hi_ready, 1)

            def seq(t):
                return t[:].rearrange("p (b s) -> p b s", b=GB)

            def gate_total(g):
                dve.wait_ge(forget_ready, g.count(1, 1))
                dve.wait_ge(inp_ready, g.count(1, 1))
                nc.vector.scalar_tensor_tensor(gate_sum[:], forget[:], EPS, inp[:], ALU.add, ALU.add)\
                    .then_inc(gate_sum_ready, 1)

            def normalize(g):
                dve.wait_ge(inv_sum_ready, g.count(1, 1))
                nc.vector.tensor_tensor(forget_norm[:], forget[:], inv_sum[:], ALU.mult).then_inc(forget_norm_ready, 1)

            def retention(g):
                dve.wait_ge(log_ret_ready, g.count(1, 1))
                if g.first:
                    dve.wait_ge(pads_ready, 4)
                if not g.first:
                    dve.wait_ge(retained_ready, g.count(1, 0))
                nc.vector.tensor_tensor_scan(log_cum[:], scan_mask[:], log_ret[:], 0.0, ALU.mult, ALU.add)\
                    .then_inc(log_cum_ready, 1)
                dve.wait_ge(log_cum_ready, g.count(1, 1))
                nc.vector.tensor_tensor(seq(log_scale), seq(log_cum)[:, :, S:PAD].to_broadcast([128, GB, S]),
                                        seq(log_cum)[:, :, 0:S], ALU.subtract).then_inc(log_scale_ready, 1)

            def recurrence(g):
                dve.wait_ge(scaled_ready, g.count(1, 1))
                nc.vector.tensor_tensor_scan(scaled_cum[:], scan_mask[:], scaled[:], 0.0, ALU.mult, ALU.add)\
                    .then_inc(scaled_cum_ready, 1)
                dve.wait_ge(scaled_cum_ready, g.count(1, 1))
                dve.wait_ge(retained_ready, g.count(1, 1))
                if not g.first:
                    dve.wait_ge(x1_ready, g.count(1, 0))
                for j in range(GB):
                    last = nc.vector.scalar_tensor_tensor(
                        hidden[:, j * S:(j + 1) * S], retained[:, j * S:(j + 1) * S], cond[:, column(g, GB, j)],
                        scaled_cum[:, j * PAD + 1:(j + 1) * PAD], ALU.mult, ALU.add)
                last.then_inc(hidden_ready, 1)

            def split_x1(g):
                dve.wait_ge(x1_ready, g.count(1, 1))
                nc.vector.tensor_copy(x1_hi[g.parity][:], x1[g.parity][:]).then_inc(x1_hi_ready, 1)

            def route_logits(g):
                dve.wait_ge(route_mm, g.count(1, 1))
                if g.first:
                    dve.wait_ge(route_cond_ready, 1)
                nc.vector.tensor_tensor(logits[:], ROUTE[:, 0:GB * E], route_cond[:, columns(g, GB * E)], ALU.add)\
                    .then_inc(logits_ready, 1)

            tt = nc.vector.tensor_tensor
            sc = score[:].rearrange("p (b e) -> p b e", b=GB)

            def wide(t):
                return t[:].unsqueeze(2).to_broadcast([128, GB, E])

            def per_expert(t):
                return t.unsqueeze(1).to_broadcast([128, GB, E])

            def gate_link(g, done):
                def link(ins, wait=True):
                    nonlocal done
                    ins.then_inc(gate_step, 1)
                    if wait:
                        dve.wait_ge(gate_step, g.count(GATE_STEPS, done))
                    done += 1
                return link

            def choose(g, link, a, src):
                link(nc.vector.tensor_reduce(t1["max" + a][:], t8[src][:], AX.X, ALU.max))
                link(tt(t8["top" + a][:], t8[src][:], wide(t1["max" + a]), ALU.is_equal))
                link(tt(t8["ranked" + a][:], t8["top" + a][:], per_expert(rank), ALU.mult))
                link(nc.vector.tensor_reduce(t1["first" + a][:], t8["ranked" + a][:], AX.X, ALU.max))
                link(tt(t8["one" + a][:], t8["ranked" + a][:], wide(t1["first" + a]), ALU.is_equal))

            def choose_first(g):
                link = gate_link(g, 1)
                dve.wait_ge(score_ready, g.count(1, 1))
                if not g.first:
                    dve.wait_ge(gates_T_mm, g.count(1, 0))
                link(tt(t8["biased"][:], sc, per_expert(route_bias), ALU.add))
                choose(g, link, "1", "biased")

            def choose_second(g):
                link = gate_link(g, 7)
                link(nc.vector.scalar_tensor_tensor(t8["rest"][:], t8["one1"][:], -BIG, t8["biased"][:],
                                                    ALU.mult, ALU.add))
                choose(g, link, "2", "rest")

            def gates_of_chosen(g):
                link = gate_link(g, 13)
                link(tt(t8["chosen"][:], t8["one1"][:], t8["one2"][:], ALU.add))
                link(tt(t8["kept"][:], t8["chosen"][:], sc, ALU.mult))
                link(nc.vector.tensor_reduce(t1["denom"][:], t8["kept"][:], AX.X, ALU.add))
                link(nc.vector.tensor_scalar(t1["denom_eps"][:], t1["denom"][:], 1e-9, None, ALU.add), wait=False)
                link(nc.vector.tensor_scalar(t1["valid"][:], t1["denom"][:], 1e-9, None, ALU.is_gt))
                link(nc.vector.reciprocal(t1["inv_denom"][:], t1["denom_eps"][:]), wait=False)
                link(nc.vector.tensor_scalar(t1["fallback"][:], t1["valid"][:], -0.5, 0.5, ALU.mult, ALU.add))
                link(tt(t1["gain_valid"][:], t1["inv_denom"][:], t1["valid"][:], ALU.mult), wait=False)
                link(tt(t8["even"][:], t8["chosen"][:], wide(t1["fallback"]), ALU.mult))
                link(tt(t8["gate_a"][:], t8["kept"][:], wide(t1["gain_valid"]), ALU.mult))
                link(tt(t8["gate"][:], t8["gate_a"][:], t8["even"][:], ALU.add))
                link(nc.vector.tensor_copy(gate_parts[:, :, 0:E], t8["gate"][:]))
                tt(gate_parts[:, :, E:2 * E], t8["gate"][:], gate_parts[:, :, 0:E].bitcast(F32), ALU.subtract)\
                    .then_inc(gate_parts_ready, 1)

            def gates_out(g):
                dve.wait_ge(gates_T_mm, g.count(1, 1))
                if not g.first:
                    dve.wait_ge(gate_mm, g.plus(-1).count(E, E))
                nc.vector.tensor_copy(gates_T[:], ROUTE[:]).then_inc(gates_T_ready, 1)

            def shared(g, s):
                dve.wait_ge(silu_ready, g.count(SU, s + 1))
                if s == 0 and not g.first:
                    dve.wait_ge(down_mm, g.plus(-1).count(E, E))
                nc.vector.scalar_tensor_tensor(h_shared[:, s, :], silu[s % 2][:], 1.0 / SHARED,
                                               PAIRS[s][1][:], ALU.mult, ALU.mult)\
                    .then_inc(h_shared_ready, 1)

            def expert(g, e):
                dve.wait_ge(gelu_ready, g.count(E, e + 1))
                dve.wait_ge(gate_mm, g.count(E, e + 1))
                if e >= 3:
                    dve.wait_ge(down_mm, g.count(E, e - 2))
                nc.vector.tensor_tensor(h_gated[e % 3][:], gelu[e % 3][:], GATE[e % 2][:], ALU.mult)\
                    .then_inc(h_gated_ready, 1)

            def residual2(g):
                dve.wait_ge(down_mm, g.count(E, E))
                if not g.first:
                    dve.wait_ge(x3_ready, g.count(1, 0))
                nc.vector.scalar_tensor_tensor(x2[:], ACC[:], 1.0 / 4, x1[g.parity][:], ALU.mult, ALU.add)\
                    .then_inc(x2_ready, 1)
                dve.wait_ge(x2_ready, g.count(1, 1))
                nc.vector.tensor_copy(x2_hi[:], x2[:]).then_inc(x2_hi_ready, 1)
                dve.wait_ge(x2_hi_ready, g.count(1, 1))
                nc.vector.tensor_tensor(x2_lo[:], x2[:], x2_hi[:].bitcast(F32), ALU.subtract).then_inc(x2_lo_ready, 1)

            def split_v(g):
                dve.wait_ge(v_loaded, g.count(16, 16))
                if not g.first:
                    dve.wait_ge(z1_mm, g.count(1, 0))
                nc.vector.tensor_copy(v_parts[:, 0, :], v_in[:]).then_inc(v_hi_ready, 1)
                dve.wait_ge(v_hi_ready, g.count(1, 1))
                nc.vector.tensor_tensor(v_parts[:, 1, :], v_in[:], v_parts[:, 0, :].bitcast(F32), ALU.subtract)\
                    .then_inc(v_lo_ready, 1)

            def mask_z1(g):
                if g.runs:
                    dve.wait_ge(z1_mm, g.count(1, 1))
                    nc.vector.tensor_tensor(z1[:], block_mask[:], LOWRANK[:], ALU.mult).then_inc(z1_ready, 1)

            setup = [0]

            def link(ins):
                setup[0] += 1
                ins.then_inc(setup_step, 1)
                dve.wait_ge(setup_step, setup[0])

            nc.vector.memset(eps_col[:], EPS).then_inc(pads_ready, 1)
            nc.vector.memset(log_ret[:], 0.0).then_inc(pads_ready, 1)
            nc.vector.memset(scaled[:], 0.0).then_inc(pads_ready, 1)
            link(nc.vector.memset(scan_mask[:], 1.0))
            nc.vector.memset(seq(scan_mask)[:, :, 0:1], 0.0).then_inc(pads_ready, 1)
            dve.wait_ge(w0_loaded, 16)
            nc.vector.tensor_copy(w_hi[:, 0:W1, :], w_raw[:, 0:W1, :]).then_inc(w0_split, 1)
            split_x(Step(0))
            dve.wait_ge(w0_split, 1)
            nc.vector.tensor_tensor(w_lo[:, 0:W1, :], w_raw[:, 0:W1, :], w_hi[:, 0:W1, :].bitcast(F32), ALU.subtract)\
                .then_inc(w0_split, 1)

            dve.wait_ge(small_loaded, 32)
            nc.vector.tensor_tensor(cond_weight[:], cond.unsqueeze(2).to_broadcast([128, B, E]),
                                    wr_raw[:, 1, :].unsqueeze(1).to_broadcast([128, B, E]), ALU.mult)\
                .then_inc(keep_ready, 1)
            nc.vector.tensor_scalar(keep[:], cond, KEEP, None, ALU.is_lt).then_inc(keep_ready, 1)
            link(nc.vector.tensor_copy(tok_f[:], tok_i[:]))
            link(nc.vector.tensor_scalar(hit_a[:], tok_f[:], index[:, 0:1], None, ALU.is_equal))
            link(nc.vector.tensor_scalar(hit_b[:], tok_f[:], index[:, 1:2], None, ALU.is_equal))
            link(nc.vector.tensor_tensor(hit_a[:], hit_a[:], hit_b[:], ALU.add))
            link(nc.vector.tensor_scalar(bias2[:], cond, biases[:, 3:4], None, ALU.add))
            link(nc.vector.tensor_copy(wr_hi[:], wr_raw[:, 0, :]))
            link(nc.vector.tensor_tensor(wr_lo[:], wr_raw[:, 0, :], wr_hi[:].bitcast(F32), ALU.subtract))

            def split_up_weights(a, b, done):
                nc.vector.tensor_copy(w_hi[:, a:b, :], w_raw[:, a:b, :]).then_inc(wup_split, 1)
                dve.wait_ge(wup_split, done + 1)
                nc.vector.tensor_tensor(w_lo[:, a:b, :], w_raw[:, a:b, :], w_hi[:, a:b, :].bitcast(F32), ALU.subtract)\
                    .then_inc(wup_split, 1)

            split_x(Step(1))
            gate_total(Step(0))
            normalize(Step(0))
            retention(Step(0))
            dve.wait_ge(wup_loaded, 64)
            split_up_weights(W1, WR, 0)
            recurrence(Step(0))
            split_x1(Step(0))
            split_x(Step(2))
            split_up_weights(WR, BLOCKS, 2)
            dve.wait_ge(kept_counted, 1)
            link(nc.vector.tensor_scalar(all_zero[:], bank[6][:, 0:B], 0.0, None, ALU.is_equal))
            link(nc.vector.tensor_tensor(hit_b[:], all_zero[:], hit_a[:], ALU.mult))
            dve.wait_ge(cond_routed, 1)
            nc.vector.tensor_copy(route_cond[:], bank[7][:, 0:B * E]).then_inc(route_cond_ready, 1)
            nc.vector.tensor_tensor(gain[:], hit_b[:], keep[:], ALU.max).then_inc(keep_ready, 1)
            dve.wait_ge(keep_ready, 3)
            dve.wait_ge(route_cond_ready, 1)
            link(nc.vector.tensor_scalar(gain[:], gain[:], 1.0, None, ALU.add))
            assert setup[0] == SETUP_STEPS
            dve.wait_ge(consts_loaded, 48)
            dve.wait_ge(consts_ready, 1)
            nc.vector.tensor_copy(eye[:], eye_raw[:]).then_inc(consts_ready, 1)
            nc.vector.tensor_copy(sel[:], sel_raw[:]).then_inc(consts_ready, 1)
            nc.vector.memset(gate_parts[:].bitcast(F32), 0.0).then_inc(consts_ready, 1)
            dve.wait_ge(consts_ready, 4)
            gate_total(Step(1))
            normalize(Step(1))
            retention(Step(1))
            route_logits(Step(0))

            def step(g):
                nxt, after_next, prev = g.plus(1), g.plus(2), g.plus(-1)
                choose_first(g)
                if not g.first:
                    split_v(prev)
                if after_next.runs:
                    gate_total(after_next)
                choose_second(g)
                shared(g, 0)
                shared(g, 1)
                shared(g, 2)
                shared(g, 3)
                gates_of_chosen(g)
                if after_next.runs:
                    normalize(after_next)
                if not g.first:
                    mask_z1(prev)
                gates_out(g)
                if after_next.runs:
                    retention(after_next)
                for e in range(E):
                    expert(g, e)
                    if e == 1 and nxt.runs:
                        recurrence(nxt)
                    if e == 3 and nxt.runs:
                        split_x1(nxt)
                    if e == 4 and g.plus(3).runs:
                        split_x(g.plus(3))
                if nxt.runs:
                    route_logits(nxt)
                residual2(g)

            step(Step(0))
            with dve.Fori(0, TURNS) as turn:
                step(Step(1, turn))
                step(Step(2, turn))
            step(Step(GROUPS - 3))
            step(Step(GROUPS - 2))
            step(Step(GROUPS - 1))
            split_v(Step(GROUPS - 1))
            mask_z1(Step(GROUPS - 1))

        @block.tensor
        def _(pe):
            def split_product(out, w, hi, lo, start=True, stop=True):
                nc.tensor.matmul(out, w_hi[:, w, :], hi, start=start, stop=False)
                nc.tensor.matmul(out, w_lo[:, w, :], hi, start=False, stop=False)
                return nc.tensor.matmul(out, w_hi[:, w, :], lo, start=False, stop=stop)

            def gates(g):
                if g.first:
                    pe.wait_ge(w0_split, 2)
                elif g.start <= 2:
                    pe.wait_ge(cand_ready, g.start)
                else:
                    pe.wait_ge(gelu_ready, g.plus(-3).count(E, E))
                pe.wait_ge(x_hi_ready, g.count(1, 1))
                pe.wait_ge(x_lo_ready, g.count(1, 1))
                for n in (WF, WI, WH):
                    split_product(bank[n][:], n, x_hi[:], x_lo[:]).then_inc(gates_mm, 1)

            def route(g):
                pe.wait_ge(x1_hi_ready, g.count(1, 1))
                pe.wait_ge(x1_lo_ready, g.count(1, 1))
                if g.first:
                    pe.wait_ge(route_cond_ready, 1)
                else:
                    pe.wait_ge(gates_T_ready, g.count(1, 0))
                for j in range(GB):
                    out = ROUTE[:, j * E:(j + 1) * E]
                    hi, lo = (t[g.parity][:, j * S:(j + 1) * S] for t in (x1_hi, x1_lo))
                    nc.tensor.matmul(out, hi, wr_hi[:], start=True, stop=False)
                    nc.tensor.matmul(out, hi, wr_lo[:], start=False, stop=False)
                    last = nc.tensor.matmul(out, lo, wr_hi[:], start=False, stop=True)
                last.then_inc(route_mm, 1)

            def shared(g):
                if g.first:
                    pe.wait_ge(wup_split, 4)
                for s in range(SU):
                    if s == 0 and not g.first:
                        pe.wait_ge(h_gated_ready, g.count(E, 0))
                    elif s == 1 and not g.first:
                        pe.wait_ge(x2_ready, g.count(1, 0))
                    elif s == 2:
                        if g.plus(2).runs:
                            pe.wait_ge(cand_ready, g.plus(2).count(1, 1))
                        else:
                            pe.wait_ge(gelu_ready, g.count(E, 0))
                    elif s == 3:
                        pe.wait_ge(silu_ready, g.count(SU, 1))
                    hi, lo = x1_hi[g.parity][:], x1_lo[g.parity][:]
                    split_product(PAIRS[s][0][:], W1 + s, hi, lo)
                    split_product(PAIRS[s][1][:], W3 + s, hi, lo).then_inc(shared_mm, 1)

            def transpose_gates(g):
                pe.wait_ge(gate_parts_ready, g.count(1, 1))
                if g.first:
                    pe.wait_ge(consts_ready, 4)
                for j in range(GB):
                    last = nc.tensor.matmul(ROUTE[:, j * S:(j + 1) * S], gate_parts[:, j, :], eye[:],
                                            start=True, stop=True)
                last.then_inc(gates_T_mm, 1)

            def low_rank(g):
                if g.runs:
                    pe.wait_ge(x2_lo_ready, g.count(1, 1))
                    pe.wait_ge(v_lo_ready, g.count(1, 1))
                    if g.plus(1).runs:
                        pe.wait_ge(silu_ready, g.plus(1).count(SU, 2))
                    v = v_parts[:].rearrange("p h k -> p (h k)")
                    nc.tensor.matmul(LOWRANK[:], v, x2_hi[:], start=True, stop=False)
                    nc.tensor.matmul(LOWRANK[:], v, x2_lo[:], start=False, stop=True).then_inc(z1_mm, 1)

            def linear(g):
                if g.runs:
                    if g.plus(1).runs:
                        pe.wait_ge(h_shared_ready, g.plus(1).count(SU, 1))
                    split_product(LINEAR[:], WL, x2_hi[:], x2_lo[:], stop=False)
                    pe.wait_ge(z1_ready, g.count(1, 1))
                    pe.wait_ge(u_loaded, g.count(32, 32))
                    nc.tensor.matmul(LINEAR[:], u_in[:], z1[:], start=False, stop=True).then_inc(linear_mm, 1)

            def up(g, e):
                if e < 3:
                    if e == 0:
                        pe.wait_ge(h_shared_ready, g.count(SU, SU))
                else:
                    pe.wait_ge(gelu_ready, g.count(E, e - 2))
                split_product(bank[e % 3][:], WR + e, x1_hi[g.parity][:], x1_lo[g.parity][:]).then_inc(expert_mm, 1)

            def spread_gate(g, e):
                if e == 0:
                    pe.wait_ge(gates_T_ready, g.count(1, 1))
                if e == 1 and not g.first:
                    pe.wait_ge(z1_ready, g.count(1, 0))
                if e >= 2:
                    pe.wait_ge(h_gated_ready, g.count(E, e - 1))
                nc.tensor.matmul(GATE[e % 2][:], sel[:, e, :], gates_T[:], start=True, stop=True).then_inc(gate_mm, 1)

            def shared_down(g):
                if g.first:
                    pe.wait_ge(down_loaded, 32)
                for s in range(SU):
                    pe.wait_ge(h_shared_ready, g.count(SU, max(s + 1, 2)))
                    nc.tensor.matmul(ACC[:], down[:, s, :], h_shared[:, s, :], start=(s == 0), stop=False)

            def expert_down(g, e):
                pe.wait_ge(h_gated_ready, g.count(E, e + 1))
                nc.tensor.matmul(ACC[:], down[:, SU + e, :], h_gated[e % 3][:], start=False, stop=(e == E - 1))\
                    .then_inc(down_mm, 1)

            def step(g):
                prev = g.plus(-1)
                if g.plus(2).runs:
                    gates(g.plus(2))
                shared(g)
                if not g.first:
                    low_rank(prev)
                shared_down(g)
                transpose_gates(g)
                if not g.first:
                    linear(prev)
                up(g, 0)
                up(g, 1)
                spread_gate(g, 0)
                for e in range(E):
                    if e + 2 < E:
                        up(g, e + 2)
                    if e + 1 < E:
                        spread_gate(g, e + 1)
                    elif g.plus(1).runs:
                        route(g.plus(1))
                    expert_down(g, e)

            gates(Step(0))
            pe.wait_ge(keep_ready, 2)
            pe.wait_ge(consts_ready, 1)
            nc.tensor.matmul(bank[6][:, 0:B], ones[:], keep[:], start=True, stop=True).then_inc(kept_counted, 1)
            nc.tensor.matmul(bank[7][:, 0:B * E], ones[:], cond_weight[:].rearrange("p b e -> p (b e)"),
                             start=True, stop=True).then_inc(cond_routed, 1)
            gates(Step(1))
            route(Step(0))
            step(Step(0))
            with pe.Fori(0, TURNS) as turn:
                step(Step(1, turn))
                step(Step(2, turn))
            step(Step(GROUPS - 3))
            step(Step(GROUPS - 2))
            step(Step(GROUPS - 1))
            low_rank(Step(GROUPS - 1))
            linear(Step(GROUPS - 1))


_OUT = (D, B * S)


def kernel(x, cond_1024, fside_Bx1x1024x16_0, itok_B_14_1018, L0_cond_W_f, L0_cond_b_f, L0_cond_W_i, L0_cond_b_i,
           L0_cond_W_h, L0_cond_b_h, L1_cond_W_router, L1_cond_router_bias, L1_cond_s_w1, L1_cond_s_w3, L1_cond_s_w2,
           L1_cond_r_w1, L1_cond_r_w2, L2_cond_W, L2_cond_fc_bias):
    import numpy as np
    import concourse.bacc as bacc
    from concourse.bass_utils import run_bass_kernel_spmd

    def lay(a, *axes):
        a = np.asarray(a)
        return np.ascontiguousarray(a.transpose(*axes) if axes else a)

    fside = np.asarray(fside_Bx1x1024x16_0)
    s_w1, s_w3, s_w2 = (np.asarray(a) for a in (L1_cond_s_w1, L1_cond_s_w3, L1_cond_s_w2))
    f = np.float32
    k = np.arange(128)
    sequence = (k % (GB * R)) // R
    block_mask = np.where(sequence[:, None] == np.arange(N)[None, :] // S, f(1.0 / (D * R)), f(0)).astype(f)
    sel = np.zeros((128, E, 128), f)
    for e in range(E):
        sel[e, e, :] = 1
        sel[E + e, e, :] = 1
    arrays = {
        "xT": lay(np.asarray(x).reshape(B * S, D), 1, 0),
        "small": np.concatenate([
            lay(cond_1024, 1, 0),
            np.stack([np.asarray(a) for a in (L0_cond_b_f, L0_cond_b_i, L0_cond_b_h, L2_cond_fc_bias)], 1),
            lay(np.asarray(L1_cond_W_router).reshape(E, 2, D), 2, 1, 0).reshape(D, 2 * E),
            np.broadcast_to(np.asarray(L1_cond_router_bias), (128, E)),
            np.stack([k, k - D], 1).astype(f),
            np.broadcast_to((E - np.arange(E)).astype(f), (128, E))], 1),
        "fsT": lay(fside[:, 0], 1, 0, 2).reshape(D, B * R),
        "fsR": lay(fside[:, 0], 0, 2, 1).reshape(B * R, D),
        "itok": lay(itok_B_14_1018),
        "gatesT": lay(np.stack([np.asarray(a) for a in (L0_cond_W_f, L0_cond_W_i, L0_cond_W_h)]), 2, 0, 1),
        "s1T": lay(s_w1.reshape(SU, 128, D), 2, 0, 1),
        "s3T": lay(s_w3.reshape(SU, 128, D), 2, 0, 1),
        "s2T": lay(s_w2.reshape(SHARED, D, 2, 128), 3, 0, 2, 1).reshape(128, SU, D),
        "r1T": lay(L1_cond_r_w1, 2, 0, 1),
        "r2T": lay(L1_cond_r_w2, 2, 0, 1),
        "wlT": lay(L2_cond_W, 1, 0),
        "c_block": block_mask,
        "c_sel": sel,
        "c_eye": np.eye(128, dtype=f),
    }
    nc = bacc.Bacc("TRN2", target_bir_lowering=False, num_devices=1)
    args = [nc.dram_tensor(f"in_{n}", a.shape, mybir.dt.from_np(a.dtype), kind="ExternalInput").ap()
            for n, a in arrays.items()]
    out = nc.dram_tensor("out_T", _OUT, mybir.dt.float32, kind="ExternalOutput").ap()
    build(nc, *args, out)
    r = run_bass_kernel_spmd(nc, [{f"in_{n}": a for n, a in arrays.items()}], core_ids=[0])
    outT = r.results[0]["out_T"]
    return np.ascontiguousarray(np.asarray(outT).reshape(D, B, S).transpose(1, 2, 0))
```

```python
import concourse.bass as bass
from concourse import mybir
from contextlib import ExitStack

B, S, D = 32, 128, 128
R = 16
E = 8
SHARED = 2
GB = 4
N = GB * S
GROUPS = B // GB
PAD = S + 1
EPS = 1e-8
KEEP = 0.8
BIG = 3.0e38
SU = SHARED * 2
WF, WI, WH = 0, 1, 2
W1, W3 = 3, 3 + SU
WR = 3 + 2 * SU
WL = WR + E
BLOCKS = WL + 1


class Step:

    def __init__(self, start, register=None, step=2):
        self.start, self.register, self.step = start, register, step

    def plus(self, n):
        return Step(self.start + n, self.register, self.step)

    @property
    def runs(self):
        return self.register is not None or 0 <= self.start < GROUPS

    @property
    def first(self):
        return self.register is None and self.start == 0

    @property
    def parity(self):
        return self.start % 2

    def count(self, per_group, k):
        if self.register is None:
            return self.start * per_group + k
        return self.register * (self.step * per_group) + (self.start * per_group + k)


LO_POOL = (1, 3)
HI_ACT = 2
LO_DVE = tuple(e for e in range(E) if e not in LO_POOL)

X_CHUNKS = ((0, 1), (1, 2), (2, 3), (3, GROUPS))

COND, BIASES, ROUTER, ROUTE_BIAS, INDEX, RANK = 0, B, B + 4, B + 4 + 2 * E, B + 4 + 3 * E, B + 6 + 3 * E
SMALL = RANK + E


def build(nc, xT, small_in, fsT, uT, itok, gatesT, s1T, s3T, s2T, r1T, r2T, wlT, c_block, c_sel, c_eye, outT):
    F32, F32R, I32 = mybir.dt.float32, mybir.dt.float32r, mybir.dt.int32
    ALU, ACT, AX = mybir.AluOpType, mybir.ActivationFunctionType, mybir.AxisListType

    with ExitStack() as ctx:
        def sb(name, shape, dt=F32):
            return ctx.enter_context(nc.sbuf_tensor(name, shape, dt))

        def sem(name):
            return ctx.enter_context(nc.semaphore(name))

        w_raw = sb("w_raw", [128, BLOCKS, 128])
        w_hi = sb("w_hi", [128, BLOCKS, 128], F32R)
        w_lo = sb("w_lo", [128, BLOCKS, 128], F32R)
        down_hi = sb("down_hi", [128, SU + E, 128], F32R)
        down_lo = sb("down_lo", [128, SU + E, 128], F32R)
        small = sb("small", [128, SMALL])
        wr_raw = small[:, ROUTER:ROUTER + 2 * E].rearrange("p (h e) -> p h e", h=2)
        wr_parts = sb("wr_parts", [128, 2 * E], F32R)
        cond = small[:, COND:COND + B]
        biases = small[:, BIASES:BIASES + 4]
        route_bias = small[:, ROUTE_BIAS:ROUTE_BIAS + E]
        rank = small[:, RANK:RANK + E]
        index = small[:, INDEX:INDEX + 2]
        cond_weight = sb("cond_weight", [128, B, E])
        block_mask = sb("block_mask", [128, N])
        sel_raw = sb("sel_raw", [2 * E, E, 128])
        sel = sb("sel", [128, E, 128], F32R)
        eye_raw = sb("eye_raw", [128, 128])
        eye = sb("eye", [128, 128], F32R)
        eps_col = sb("eps_col", [128, 1])
        ones = sb("ones", [128, 128])
        scan_mask = sb("scan_mask", [128, GB * PAD])
        tok_i = sb("tok_i", [128, B], I32)
        tok_f = sb("tok_f", [128, B])
        keep = sb("keep", [128, B])
        all_zero = sb("all_zero", [128, B])
        hit_a = sb("hit_a", [128, B])
        hit_b = sb("hit_b", [128, B])
        gain = sb("gain", [128, B])
        bias2 = sb("bias2", [128, B])
        route_cond = sb("route_cond", [128, B * E])

        x_all = sb("x_all", [128, B * S])
        x_hi = sb("x_hi", [128, N], F32R)
        x_lo = sb("x_lo", [128, N], F32R)
        forget = sb("forget", [128, N])
        inp = sb("inp", [128, N])
        cand = sb("cand", [128, N])
        gate_sum = sb("gate_sum", [128, N])
        log_sum = sb("log_sum", [128, N])
        inv_sum = sb("inv_sum", [128, N])
        forget_norm = sb("forget_norm", [128, N])
        input_norm = sb("input_norm", [128, N])
        new_info = sb("new_info", [128, N])
        log_ret = sb("log_ret", [128, GB * PAD])
        log_cum = sb("log_cum", [128, GB * PAD])
        log_scale = sb("log_scale", [128, N])
        scaling = sb("scaling", [128, N])
        retained = sb("retained", [128, N])
        scaled = sb("scaled", [128, GB * PAD])
        scaled_cum = sb("scaled_cum", [128, GB * PAD])
        hidden = sb("hidden", [128, N])
        x1 = [sb(f"x1_{p}", [128, N]) for p in range(2)]
        x1_hi = [sb(f"x1_hi{p}", [128, N], F32R) for p in range(2)]
        x1_lo = [sb(f"x1_lo{p}", [128, N], F32R) for p in range(2)]

        low_logits = sb("low_logits", [128, GB, E])
        logits = sb("logits", [128, GB * E])
        score = sb("score", [128, GB * E])
        t8 = {n: sb(n, [128, GB, E]) for n in
              ("biased", "top1", "ranked1", "one1", "rest", "top2", "ranked2", "one2", "chosen", "kept", "even",
               "gate_a", "gate")}
        t1 = {n: sb(n, [128, GB]) for n in
              ("max1", "first1", "max2", "first2", "denom", "denom_eps", "inv_denom", "valid", "gain_valid",
               "fallback")}
        gate_parts = sb("gate_parts", [128, GB, 128], F32R)
        gates_T = sb("gates_T", [128, N], F32R)
        silu = [sb(f"silu{p}", [128, N]) for p in range(2)]
        h_shared = sb("h_shared", [128, SU, N])
        down = h_shared[:].rearrange("p s n -> p (s n)")[:, 0:(SU + E) * 128].rearrange("p (k n) -> p k n", n=128)
        shared_hi = sb("shared_hi", [128, SU, N], F32R)
        shared_lo = sb("shared_lo", [128, SU, N], F32R)
        gelu = [sb(f"gelu{p}", [128, N]) for p in range(3)]
        h_gated = [sb(f"h_gated{p}", [128, N]) for p in range(4)]
        h_hi = [sb(f"h_hi{p}", [128, N], F32R) for p in range(4)]
        h_lo = [sb(f"h_lo{p}", [128, N], F32R) for p in range(4)]
        x2 = sb("x2", [128, N])
        x2_hi = sb("x2_hi", [128, N], F32R)
        x2_lo = sb("x2_lo", [128, N], F32R)

        v_all = sb("v_all", [128, B * R])
        v_parts = sb("v_parts", [128, 2, GB * R], F32R)
        u_in = sb("u_in", [128, D])
        z1 = sb("z1", [128, N])
        act2 = sb("act2", [128, N])
        x3 = sb("x3", [128, N])
        out_sb = sb("out_sb", [128, N])

        bank = [ctx.enter_context(nc.psum_tensor(f"bank{i}", [128, N], F32)) for i in range(8)]
        ACC, ROUTE, LOWRANK, LINEAR = bank[5], bank[6], bank[7], bank[4]
        GATE = (bank[3], bank[7])
        PAIRS = ((bank[3], bank[4]), (bank[7], bank[5]), (bank[0], bank[1]), (bank[2], bank[3]))

        w0_loaded, wup_loaded, down_loaded = sem("w0_loaded"), sem("wup_loaded"), sem("down_loaded")
        small_loaded, consts_loaded, mask_loaded = sem("small_loaded"), sem("consts_loaded"), sem("mask_loaded")
        x_loaded = [sem(f"x{c}_loaded") for c in range(len(X_CHUNKS))]
        v_loaded, u_loaded, out_stored = sem("v_loaded"), sem("u_loaded"), sem("out_stored")
        w0_split, shared_split, routed_split = sem("w0_split"), sem("shared_split"), sem("routed_split")
        consts_ready = sem("consts_ready")
        ones_ready, sel_cleared = sem("ones_ready"), sem("sel_cleared")
        pads_ready, keep_ready, kept_counted = sem("pads_ready"), sem("keep_ready"), sem("kept_counted")
        setup_step, cond_routed, route_cond_ready = sem("setup_step"), sem("cond_routed"), sem("route_cond_ready")
        x_hi_ready, x_lo_ready, gates_mm = sem("x_hi_ready"), sem("x_lo_ready"), sem("gates_mm")
        forget_ready, inp_ready, cand_ready = sem("forget_ready"), sem("inp_ready"), sem("cand_ready")
        gate_sum_ready, log_sum_ready, inv_sum_ready = sem("gate_sum_ready"), sem("log_sum_ready"), sem("inv_sum_ready")
        forget_norm_ready, input_norm_ready = sem("forget_norm_ready"), sem("input_norm_ready")
        new_info_ready, log_ret_ready, log_cum_ready = sem("new_info_ready"), sem("log_ret_ready"), sem("log_cum_ready")
        log_scale_ready, scaling_ready, retained_ready = sem("log_scale_ready"), sem("scaling_ready"), sem("retained_ready")
        scaled_ready, scaled_cum_ready, hidden_ready = sem("scaled_ready"), sem("scaled_cum_ready"), sem("hidden_ready")
        x1_ready, x1_hi_ready, x1_lo_ready = sem("x1_ready"), sem("x1_hi_ready"), sem("x1_lo_ready")
        route_mm, low_logits_ready = sem("route_mm"), sem("low_logits_ready")
        logits_ready, score_ready = sem("logits_ready"), sem("score_ready")
        gate_step, gate_parts_ready = sem("gate_step"), sem("gate_parts_ready")
        gates_T_mm, gates_T_ready = sem("gates_T_mm"), sem("gates_T_ready")
        shared_mm, silu_ready, h_shared_ready = sem("shared_mm"), sem("silu_ready"), sem("h_shared_ready")
        expert_mm, gate_mm, gelu_ready = sem("expert_mm"), sem("gate_mm"), sem("gelu_ready")
        h_gated_ready, down_mm = sem("h_gated_ready"), sem("down_mm")
        h_hi_ready, h_lo_pool_ready, h_lo_dve_ready = sem("h_hi_ready"), sem("h_lo_pool_ready"), sem("h_lo_dve_ready")
        down_split, shared_lo_ready = sem("down_split"), sem("shared_lo_ready")
        shared_hi_act_ready, shared_hi_dve_ready = sem("shared_hi_act_ready"), sem("shared_hi_dve_ready")
        x2_ready, x2_hi_ready, x2_lo_ready = sem("x2_ready"), sem("x2_hi_ready"), sem("x2_lo_ready")
        v_hi_ready, v_lo_ready = sem("v_hi_ready"), sem("v_lo_ready")
        z1_mm, z1_ready, linear_mm, act2_ready = sem("z1_mm"), sem("z1_ready"), sem("linear_mm"), sem("act2_ready")
        x3_ready, out_ready = sem("x3_ready"), sem("out_ready")

        def wait_x(engine, g):
            starts = [a for a, _ in X_CHUNKS]
            if g.start in starts:
                engine.wait_ge(x_loaded[starts.index(g.start)], 16)

        def wait_shared_hi(engine, g, s):
            if s < HI_ACT:
                engine.wait_ge(shared_hi_act_ready, g.count(HI_ACT, s + 1))
            else:
                engine.wait_ge(shared_hi_dve_ready, g.count(SU - HI_ACT, s - HI_ACT + 1))

        def wait_h_lo(engine, g, e):
            for mine, signal in ((LO_POOL, h_lo_pool_ready), (LO_DVE, h_lo_dve_ready)):
                if e % E in mine:
                    k = mine.index(e % E) + 1
                    engine.wait_ge(signal, g.count(len(mine), k if e >= 0 else k - len(mine)))

        block = ctx.enter_context(nc.Block())

        GATE_STEPS = 24
        SETUP_STEPS = 11

        TURNS = (GROUPS - 4) // 2

        def columns(g, width):
            return bass.ds(g.count(width, 0), width)

        def column(g, per_group, j):
            return bass.ds(g.count(per_group, j), 1)

        @block.sync
        def _(sp):
            def step(g):
                if not g.first:
                    sp.wait_ge(out_ready, g.count(1, 0))
                    sp.dma_start(u_in[:], uT[:, columns(g, D)]).then_inc(u_loaded, 16)
                    sp.dma_start(outT[:, columns(g.plus(-1), N)], out_sb[:]).then_inc(out_stored, 16)

            def load_x(c):
                a, b = X_CHUNKS[c]
                sp.dma_start(x_all[:, a * N:b * N], xT[:, a * N:b * N]).then_inc(x_loaded[c], 16)

            load_x(0)
            sp.dma_start(w_raw[:, 0:W1, :], gatesT).then_inc(w0_loaded, 16)
            load_x(1)
            sp.dma_start(w_raw[:, W1:W3, :], s1T).then_inc(wup_loaded, 16)
            sp.dma_start(w_raw[:, W3:WR, :], s3T).then_inc(wup_loaded, 16)
            sp.dma_start(sel_raw[:], c_sel).then_inc(consts_loaded, 16)
            sp.dma_start(eye_raw[:], c_eye).then_inc(consts_loaded, 16)
            load_x(2)
            sp.dma_start(w_raw[:, WR:WL, :], r1T).then_inc(wup_loaded, 16)
            sp.dma_start(w_raw[:, WL, :], wlT).then_inc(wup_loaded, 16)
            sp.dma_start(down[:, 0:SU], s2T).then_inc(down_loaded, 16)
            sp.dma_start(down[:, SU:], r2T).then_inc(down_loaded, 16)
            sp.dma_start(v_all[:], fsT).then_inc(v_loaded, 16)
            sp.dma_start(block_mask[:], c_block).then_inc(mask_loaded, 16)
            sp.dma_start(u_in[:], uT[:, 0:D]).then_inc(u_loaded, 16)
            load_x(3)

            step(Step(0))
            with sp.Fori(0, TURNS) as turn:
                step(Step(1, turn))
                step(Step(2, turn))
            step(Step(GROUPS - 3))
            step(Step(GROUPS - 2))
            step(Step(GROUPS - 1))
            sp.wait_ge(out_ready, GROUPS)
            sp.dma_start(outT[:, (GROUPS - 1) * N:GROUPS * N], out_sb[:]).then_inc(out_stored, 16)
            sp.wait_ge(out_stored, 16 * (GROUPS + 1))

        @block.scalar
        def _(act):
            nc.scalar.preload_act_table_set("sigmoid_and_others")
            act.dma_start(small[:], small_in).then_inc(small_loaded, 16)
            act.dma_start(tok_i[:], itok.partition_broadcast(128)).then_inc(small_loaded, 16)

            def gates(g):
                if g.first:
                    act.wait_ge(small_loaded, 32)
                act.wait_ge(gates_mm, g.count(3, 1))
                nc.scalar.activation(forget[:], bank[0][:], ACT.Sigmoid, bias=biases[:, 0:1]).then_inc(forget_ready, 1)
                act.wait_ge(gates_mm, g.count(3, 2))
                if not g.first:
                    act.wait_ge(input_norm_ready, g.count(1, 0))
                nc.scalar.activation(inp[:], bank[1][:], ACT.Sigmoid, bias=biases[:, 1:2]).then_inc(inp_ready, 1)
                act.wait_ge(gates_mm, g.count(3, 3))
                if not g.first:
                    act.wait_ge(new_info_ready, g.count(1, 0))
                nc.scalar.activation(cand[:], bank[2][:], ACT.Identity, bias=biases[:, 2:3]).then_inc(cand_ready, 1)

            def logs(g, before):
                nc.scalar.preload_act_table_set("natural_log_exp_and_others")
                if g.runs:
                    act.wait_ge(gate_sum_ready, g.count(1, 1))
                    if g.first:
                        act.wait_ge(pads_ready, 4)
                    nc.scalar.activation(log_sum[:], gate_sum[:], ACT.Ln, bias=eps_col[:, 0:1]).then_inc(log_sum_ready, 1)
                    act.wait_ge(log_sum_ready, g.count(1, 1))
                    nc.scalar.activation(inv_sum[:], log_sum[:], ACT.Exp, scale=-1.0).then_inc(inv_sum_ready, 1)
                if before.runs:
                    act.wait_ge(log_scale_ready, before.count(1, 1))
                    nc.scalar.activation(scaling[:], log_scale[:], ACT.Exp).then_inc(scaling_ready, 1)
                    nc.scalar.activation(retained[:].rearrange("p (b s) -> p b s", b=GB),
                                         log_cum[:].rearrange("p (b s) -> p b s", b=GB)[:, :, 1:PAD],
                                         ACT.Exp).then_inc(retained_ready, 1)
                if g.runs:
                    act.wait_ge(forget_norm_ready, g.count(1, 1))
                    nc.scalar.activation(log_ret[:].rearrange("p (b s) -> p b s", b=GB)[:, :, 1:PAD],
                                         forget_norm[:].rearrange("p (b s) -> p b s", b=GB),
                                         ACT.Ln, bias=eps_col[:, 0:1]).then_inc(log_ret_ready, 1)

            def scores(g):
                nc.scalar.preload_act_table_set("sigmoid_and_others")
                act.wait_ge(logits_ready, g.count(1, 1))
                nc.scalar.activation(score[:], logits[:], ACT.Sigmoid).then_inc(score_ready, 1)

            def shared_high(g, s):
                act.wait_ge(h_shared_ready, g.count(SU, s + 1))
                if s == 0 and not g.first:
                    act.wait_ge(down_mm, g.count(E, 0))
                nc.scalar.activation(shared_hi[:, s, :], h_shared[:, s, :], ACT.Copy).then_inc(shared_hi_act_ready, 1)

            def shared(g):
                nc.scalar.preload_act_table_set("silu_and_others")
                for s in range(SU):
                    act.wait_ge(shared_mm, g.count(SU, s + 1))
                    if s >= 2 or not g.first:
                        act.wait_ge(h_shared_ready, g.count(SU, s - 1))
                    nc.scalar.activation(silu[s % 2][:], PAIRS[s][0][:], ACT.Silu).then_inc(silu_ready, 1)
                    if 1 <= s <= HI_ACT:
                        shared_high(g, s - 1)

            def high_part(g, e):
                act.wait_ge(h_gated_ready, g.count(E, e + 1))
                if e >= 4 or not g.first:
                    act.wait_ge(down_mm, g.count(E, e - 3))
                nc.scalar.activation(h_hi[e % 4][:], h_gated[e % 4][:], ACT.Copy).then_inc(h_hi_ready, 1)

            def experts(g, prev):
                for e in range(E):
                    if e == 3:
                        linear(prev)
                    act.wait_ge(expert_mm, g.count(E, e + 1))
                    if e >= 3:
                        act.wait_ge(h_gated_ready, g.count(E, e - 2))
                    elif e == 0 and not g.first:
                        act.wait_ge(h_gated_ready, g.count(E, 0))
                    nc.scalar.activation(gelu[e % 3][:], bank[e % 3][:], ACT.Gelu).then_inc(gelu_ready, 1)
                    if e >= 1:
                        high_part(g, e - 1)
                high_part(g, E - 1)

            def linear(g):
                if g.runs:
                    if g.first:
                        act.wait_ge(setup_step, SETUP_STEPS)
                    act.wait_ge(linear_mm, g.count(1, 1))
                    if not g.first:
                        act.wait_ge(x3_ready, g.count(1, 0))
                    for j in range(GB):
                        last = nc.scalar.activation(act2[:, j * S:(j + 1) * S], LINEAR[:, j * S:(j + 1) * S], ACT.Gelu,
                                                    bias=bias2[:, column(g, GB, j)])
                    last.then_inc(act2_ready, 1)

            def step(g):
                scores(g)
                if g.plus(2).runs:
                    gates(g.plus(2))
                shared(g)
                if g.plus(1).runs:
                    logs(g.plus(2), g.plus(1))
                nc.scalar.preload_act_table_set("gelu_and_others")
                experts(g, g.plus(-1))

            gates(Step(0))
            logs(Step(0), Step(-1))
            logs(Step(-1), Step(0))
            nc.scalar.preload_act_table_set("sigmoid_and_others")
            gates(Step(1))
            logs(Step(1), Step(-1))
            step(Step(0))
            with act.Fori(0, TURNS) as turn:
                step(Step(1, turn))
                step(Step(2, turn))
            step(Step(GROUPS - 3))
            step(Step(GROUPS - 2))
            step(Step(GROUPS - 1))
            linear(Step(GROUPS - 1))

        @block.gpsimd
        def _(pool):
            nc.gpsimd.memset(ones[:], 1.0).then_inc(ones_ready, 1)
            nc.gpsimd.memset(sel[:].bitcast(F32), 0.0).then_inc(sel_cleared, 1)
            nc.gpsimd.memset(out_sb[:], 0.0).then_inc(out_stored, 16)

            def split_x(g):
                wait_x(pool, g)
                pool.wait_ge(x_hi_ready, g.count(1, 1))
                if not g.first:
                    pool.wait_ge(gates_mm, g.plus(-1).count(3, 3))
                nc.gpsimd.tensor_tensor(x_lo[:], x_all[:, columns(g, N)], x_hi[:].bitcast(F32), ALU.subtract)\
                    .then_inc(x_lo_ready, 1)

            def low_part(g, e):
                pool.wait_ge(h_hi_ready, g.count(E, e + 1))
                nc.gpsimd.tensor_tensor(h_lo[e % 4][:], h_gated[e % 4][:], h_hi[e % 4][:].bitcast(F32), ALU.subtract)\
                    .then_inc(h_lo_pool_ready, 1)

            def shared_low(g, s):
                wait_shared_hi(pool, g, s)
                nc.gpsimd.tensor_tensor(shared_lo[:, s, :], h_shared[:, s, :], shared_hi[:, s, :].bitcast(F32),
                                        ALU.subtract).then_inc(shared_lo_ready, 1)

            def input_norms(g):
                pool.wait_ge(inv_sum_ready, g.count(1, 1))
                pool.wait_ge(inp_ready, g.count(1, 1))
                nc.gpsimd.tensor_tensor(input_norm[:], inp[:], inv_sum[:], ALU.mult).then_inc(input_norm_ready, 1)

            def new_infos(g):
                pool.wait_ge(input_norm_ready, g.count(1, 1))
                pool.wait_ge(cand_ready, g.count(1, 1))
                if not g.first:
                    pool.wait_ge(scaled_ready, g.count(1, 0))
                nc.gpsimd.tensor_tensor(new_info[:], input_norm[:], cand[:], ALU.mult).then_inc(new_info_ready, 1)

            def scale(g):
                pool.wait_ge(scaling_ready, g.count(1, 1))
                pool.wait_ge(new_info_ready, g.count(1, 1))
                if g.first:
                    pool.wait_ge(pads_ready, 4)
                nc.gpsimd.tensor_tensor(scaled[:].rearrange("p (b s) -> p b s", b=GB)[:, :, 1:PAD],
                                        scaling[:].rearrange("p (b s) -> p b s", b=GB),
                                        new_info[:].rearrange("p (b s) -> p b s", b=GB), ALU.mult)\
                    .then_inc(scaled_ready, 1)

            def residual1(g):
                pool.wait_ge(hidden_ready, g.count(1, 1))
                nc.gpsimd.tensor_tensor(x1[g.parity][:], hidden[:], x_all[:, columns(g, N)], ALU.add).then_inc(x1_ready, 1)

            def split_x1(g):
                pool.wait_ge(x1_hi_ready, g.count(1, 1))
                nc.gpsimd.tensor_tensor(x1_lo[g.parity][:], x1[g.parity][:], x1_hi[g.parity][:].bitcast(F32),
                                        ALU.subtract).then_inc(x1_lo_ready, 1)

            def split_x2(g):
                pool.wait_ge(x2_hi_ready, g.count(1, 1))
                nc.gpsimd.tensor_tensor(x2_lo[:], x2[:], x2_hi[:].bitcast(F32), ALU.subtract).then_inc(x2_lo_ready, 1)

            def gate_total(g):
                pool.wait_ge(forget_ready, g.count(1, 1))
                pool.wait_ge(inp_ready, g.count(1, 1))
                if not g.first:
                    pool.wait_ge(log_sum_ready, g.count(1, 0))
                nc.gpsimd.tensor_tensor(gate_sum[:], forget[:], inp[:], ALU.add).then_inc(gate_sum_ready, 1)

            def output(g):
                if g.runs:
                    pool.wait_ge(act2_ready, g.count(1, 1))
                    pool.wait_ge(x2_ready, g.count(1, 1))
                    nc.gpsimd.tensor_tensor(x3[:], x2[:], act2[:], ALU.add).then_inc(x3_ready, 1)
                    pool.wait_ge(x3_ready, g.count(1, 1))
                    pool.wait_ge(out_stored, g.count(16, 16))
                    if g.first:
                        pool.wait_ge(setup_step, SETUP_STEPS)
                    nc.gpsimd.tensor_tensor(out_sb[:].rearrange("p (b s) -> p b s", b=GB),
                                            x3[:].rearrange("p (b s) -> p b s", b=GB),
                                            gain[:, columns(g, GB)].unsqueeze(2).to_broadcast([128, GB, S]),
                                            ALU.mult).then_inc(out_ready, 1)

            def step(g):
                nxt, after_next = g.plus(1), g.plus(2)
                if after_next.runs:
                    gate_total(after_next)
                for s in range(SU - 1):
                    shared_low(g, s)
                if nxt.runs:
                    scale(nxt)
                shared_low(g, SU - 1)
                if after_next.runs:
                    input_norms(after_next)
                    new_infos(after_next)
                low_part(g, LO_POOL[0])
                if nxt.runs:
                    residual1(nxt)
                low_part(g, LO_POOL[1])
                if nxt.runs:
                    split_x1(nxt)
                if g.plus(3).runs:
                    split_x(g.plus(3))
                if not g.first:
                    output(g.plus(-1))
                if nxt.runs:
                    split_x2(g)

            pool.wait_ge(w0_split, 1)
            nc.gpsimd.tensor_tensor(w_lo[:, 0:W1, :], w_raw[:, 0:W1, :], w_hi[:, 0:W1, :].bitcast(F32), ALU.subtract)\
                .then_inc(w0_split, 1)
            split_x(Step(1))
            input_norms(Step(0))
            new_infos(Step(0))
            scale(Step(0))
            split_x(Step(2))
            pool.wait_ge(routed_split, 1)
            nc.gpsimd.tensor_tensor(w_lo[:, WR:BLOCKS, :], w_raw[:, WR:BLOCKS, :], w_hi[:, WR:BLOCKS, :].bitcast(F32),
                                    ALU.subtract).then_inc(routed_split, 1)
            input_norms(Step(1))
            new_infos(Step(1))
            pool.wait_ge(down_split, 1)
            nc.gpsimd.tensor_tensor(down_lo[:], down, down_hi[:].bitcast(F32), ALU.subtract)\
                .then_inc(down_split, 1)
            step(Step(0))
            with pool.Fori(0, TURNS) as turn:
                step(Step(1, turn))
                step(Step(2, turn))
            step(Step(GROUPS - 3))
            step(Step(GROUPS - 2))
            step(Step(GROUPS - 1))

        @block.vector
        def _(dve):
            def split_x(g):
                wait_x(dve, g)
                if not g.first:
                    dve.wait_ge(gates_mm, g.plus(-1).count(3, 3))
                nc.vector.tensor_copy(x_hi[:], x_all[:, columns(g, N)]).then_inc(x_hi_ready, 1)

            def seq(t):
                return t[:].rearrange("p (b s) -> p b s", b=GB)

            def normalize(g):
                dve.wait_ge(inv_sum_ready, g.count(1, 1))
                nc.vector.tensor_tensor(forget_norm[:], forget[:], inv_sum[:], ALU.mult).then_inc(forget_norm_ready, 1)

            def retention(g):
                dve.wait_ge(log_ret_ready, g.count(1, 1))
                if g.first:
                    dve.wait_ge(pads_ready, 4)
                if not g.first:
                    dve.wait_ge(retained_ready, g.count(1, 0))
                nc.vector.tensor_tensor_scan(log_cum[:], scan_mask[:], log_ret[:], 0.0, ALU.mult, ALU.add)\
                    .then_inc(log_cum_ready, 1)
                dve.wait_ge(log_cum_ready, g.count(1, 1))
                nc.vector.tensor_tensor(seq(log_scale), seq(log_cum)[:, :, S:PAD].to_broadcast([128, GB, S]),
                                        seq(log_cum)[:, :, 0:S], ALU.subtract).then_inc(log_scale_ready, 1)

            def scaled_sum(g):
                dve.wait_ge(scaled_ready, g.count(1, 1))
                nc.vector.tensor_tensor_scan(scaled_cum[:], scan_mask[:], scaled[:], 0.0, ALU.mult, ALU.add)\
                    .then_inc(scaled_cum_ready, 1)

            def hidden_state(g):
                dve.wait_ge(scaled_cum_ready, g.count(1, 1))
                dve.wait_ge(retained_ready, g.count(1, 1))
                if not g.first:
                    dve.wait_ge(x1_ready, g.count(1, 0))
                for j in range(GB):
                    last = nc.vector.scalar_tensor_tensor(
                        hidden[:, j * S:(j + 1) * S], retained[:, j * S:(j + 1) * S], cond[:, column(g, GB, j)],
                        scaled_cum[:, j * PAD + 1:(j + 1) * PAD], ALU.mult, ALU.add)
                last.then_inc(hidden_ready, 1)

            def split_x1(g):
                dve.wait_ge(x1_ready, g.count(1, 1))
                nc.vector.tensor_copy(x1_hi[g.parity][:], x1[g.parity][:]).then_inc(x1_hi_ready, 1)

            def route_logits(g):
                dve.wait_ge(route_mm, g.count(1, 1))
                if g.first:
                    dve.wait_ge(route_cond_ready, 1)
                parts = ROUTE[:, 0:2 * GB * E].rearrange("p (b h e) -> p b h e", b=GB, h=2)
                nc.vector.tensor_tensor(low_logits[:], parts[:, :, 1, :],
                                        route_cond[:, columns(g, GB * E)].rearrange("p (b e) -> p b e", b=GB), ALU.add)\
                    .then_inc(low_logits_ready, 1)
                dve.wait_ge(low_logits_ready, g.count(1, 1))
                nc.vector.tensor_tensor(logits[:].rearrange("p (b e) -> p b e", b=GB), parts[:, :, 0, :],
                                        low_logits[:], ALU.add).then_inc(logits_ready, 1)

            tt = nc.vector.tensor_tensor

            def low_part(g, e):
                if e in LO_DVE:
                    dve.wait_ge(h_hi_ready, g.count(E, e + 1))
                    tt(h_lo[e % 4][:], h_gated[e % 4][:], h_hi[e % 4][:].bitcast(F32), ALU.subtract)\
                        .then_inc(h_lo_dve_ready, 1)
            sc = score[:].rearrange("p (b e) -> p b e", b=GB)

            def wide(t):
                return t[:].unsqueeze(2).to_broadcast([128, GB, E])

            def per_expert(t):
                return t.unsqueeze(1).to_broadcast([128, GB, E])

            def gate_link(g, done):
                def link(ins, wait=True):
                    nonlocal done
                    ins.then_inc(gate_step, 1)
                    if wait:
                        dve.wait_ge(gate_step, g.count(GATE_STEPS, done))
                    done += 1
                return link

            def choose(g, link, a, src):
                link(nc.vector.tensor_reduce(t1["max" + a][:], t8[src][:], AX.X, ALU.max))
                link(tt(t8["top" + a][:], t8[src][:], wide(t1["max" + a]), ALU.is_equal))
                link(tt(t8["ranked" + a][:], t8["top" + a][:], per_expert(rank), ALU.mult))
                link(nc.vector.tensor_reduce(t1["first" + a][:], t8["ranked" + a][:], AX.X, ALU.max))
                link(tt(t8["one" + a][:], t8["ranked" + a][:], wide(t1["first" + a]), ALU.is_equal))

            def choose_first(g):
                link = gate_link(g, 1)
                dve.wait_ge(score_ready, g.count(1, 1))
                if not g.first:
                    dve.wait_ge(gates_T_mm, g.count(1, 0))
                link(tt(t8["biased"][:], sc, per_expert(route_bias), ALU.add))
                choose(g, link, "1", "biased")

            def choose_second(g):
                link = gate_link(g, 7)
                link(nc.vector.scalar_tensor_tensor(t8["rest"][:], t8["one1"][:], -BIG, t8["biased"][:],
                                                    ALU.mult, ALU.add))
                choose(g, link, "2", "rest")

            def chosen_sum(g):
                link = gate_link(g, 13)
                link(tt(t8["chosen"][:], t8["one1"][:], t8["one2"][:], ALU.add))
                link(tt(t8["kept"][:], t8["chosen"][:], sc, ALU.mult))
                link(nc.vector.tensor_reduce(t1["denom"][:], t8["kept"][:], AX.X, ALU.add))

            def gates_of_chosen(g):
                link = gate_link(g, 16)
                link(nc.vector.tensor_scalar(t1["denom_eps"][:], t1["denom"][:], 1e-9, None, ALU.add), wait=False)
                link(nc.vector.tensor_scalar(t1["valid"][:], t1["denom"][:], 1e-9, None, ALU.is_gt))
                link(nc.vector.reciprocal(t1["inv_denom"][:], t1["denom_eps"][:]), wait=False)
                link(nc.vector.tensor_scalar(t1["fallback"][:], t1["valid"][:], -0.5, 0.5, ALU.mult, ALU.add))
                link(tt(t1["gain_valid"][:], t1["inv_denom"][:], t1["valid"][:], ALU.mult), wait=False)
                link(tt(t8["even"][:], t8["chosen"][:], wide(t1["fallback"]), ALU.mult))
                link(tt(t8["gate_a"][:], t8["kept"][:], wide(t1["gain_valid"]), ALU.mult))
                link(tt(t8["gate"][:], t8["gate_a"][:], t8["even"][:], ALU.add))
                link(nc.vector.tensor_copy(gate_parts[:, :, 0:E], t8["gate"][:]))
                tt(gate_parts[:, :, E:2 * E], t8["gate"][:], gate_parts[:, :, 0:E].bitcast(F32), ALU.subtract)\
                    .then_inc(gate_parts_ready, 1)

            def gates_out(g):
                dve.wait_ge(gates_T_mm, g.count(1, 1))
                if not g.first:
                    dve.wait_ge(gate_mm, g.plus(-1).count(E, E))
                nc.vector.tensor_copy(gates_T[:], ROUTE[:]).then_inc(gates_T_ready, 1)

            def shared(g, s):
                dve.wait_ge(silu_ready, g.count(SU, s + 1))
                if g.first:
                    dve.wait_ge(down_split, 2)
                else:
                    dve.wait_ge(shared_lo_ready, g.count(SU, s + 1 - SU))
                nc.vector.scalar_tensor_tensor(h_shared[:, s, :], silu[s % 2][:], 1.0 / SHARED,
                                               PAIRS[s][1][:], ALU.mult, ALU.mult)\
                    .then_inc(h_shared_ready, 1)

            def shared_high(g, s):
                dve.wait_ge(h_shared_ready, g.count(SU, s + 1))
                if s == HI_ACT and not g.first:
                    dve.wait_ge(down_mm, g.count(E, 0))
                nc.vector.tensor_copy(shared_hi[:, s, :], h_shared[:, s, :]).then_inc(shared_hi_dve_ready, 1)

            def expert(g, e):
                dve.wait_ge(gelu_ready, g.count(E, e + 1))
                dve.wait_ge(gate_mm, g.count(E, e + 1))
                if e >= 4 or not g.first:
                    wait_h_lo(dve, g, e - 4)
                nc.vector.tensor_tensor(h_gated[e % 4][:], gelu[e % 3][:], GATE[e % 2][:], ALU.mult)\
                    .then_inc(h_gated_ready, 1)

            def residual2(g):
                dve.wait_ge(down_mm, g.count(E, E))
                if not g.first:
                    dve.wait_ge(x3_ready, g.count(1, 0))
                nc.vector.scalar_tensor_tensor(x2[:], ACC[:], 1.0 / 4, x1[g.parity][:], ALU.mult, ALU.add)\
                    .then_inc(x2_ready, 1)
                dve.wait_ge(x2_ready, g.count(1, 1))
                nc.vector.tensor_copy(x2_hi[:], x2[:]).then_inc(x2_hi_ready, 1)

            def split_v(g):
                if g.first:
                    dve.wait_ge(v_loaded, 16)
                else:
                    dve.wait_ge(z1_mm, g.count(1, 0))
                nc.vector.tensor_copy(v_parts[:, 0, :], v_all[:, columns(g, GB * R)]).then_inc(v_hi_ready, 1)
                dve.wait_ge(v_hi_ready, g.count(1, 1))
                nc.vector.tensor_tensor(v_parts[:, 1, :], v_all[:, columns(g, GB * R)], v_parts[:, 0, :].bitcast(F32), ALU.subtract)\
                    .then_inc(v_lo_ready, 1)

            def mask_z1(g):
                if g.runs:
                    if g.first:
                        dve.wait_ge(mask_loaded, 16)
                    dve.wait_ge(z1_mm, g.count(1, 1))
                    nc.vector.tensor_tensor(z1[:], block_mask[:], LOWRANK[:], ALU.mult).then_inc(z1_ready, 1)

            setup = [0]

            def link(ins):
                setup[0] += 1
                ins.then_inc(setup_step, 1)
                dve.wait_ge(setup_step, setup[0])

            nc.vector.memset(eps_col[:], EPS).then_inc(pads_ready, 1)
            nc.vector.memset(log_ret[:], 0.0).then_inc(pads_ready, 1)
            nc.vector.memset(scaled[:], 0.0).then_inc(pads_ready, 1)
            link(nc.vector.memset(scan_mask[:], 1.0))
            nc.vector.memset(seq(scan_mask)[:, :, 0:1], 0.0).then_inc(pads_ready, 1)
            dve.wait_ge(w0_loaded, 16)
            nc.vector.tensor_copy(w_hi[:, 0:W1, :], w_raw[:, 0:W1, :]).then_inc(w0_split, 1)
            split_x(Step(0))
            dve.wait_ge(x_hi_ready, 1)
            nc.vector.tensor_tensor(x_lo[:], x_all[:, 0:N], x_hi[:].bitcast(F32), ALU.subtract).then_inc(x_lo_ready, 1)

            dve.wait_ge(small_loaded, 32)
            nc.vector.tensor_tensor(cond_weight[:], cond.unsqueeze(2).to_broadcast([128, B, E]),
                                    wr_raw[:, 1, :].unsqueeze(1).to_broadcast([128, B, E]), ALU.mult)\
                .then_inc(keep_ready, 1)
            nc.vector.tensor_scalar(keep[:], cond, KEEP, None, ALU.is_lt).then_inc(keep_ready, 1)
            link(nc.vector.tensor_copy(tok_f[:], tok_i[:]))
            link(nc.vector.tensor_scalar(hit_a[:], tok_f[:], index[:, 0:1], None, ALU.is_equal))
            link(nc.vector.tensor_scalar(hit_b[:], tok_f[:], index[:, 1:2], None, ALU.is_equal))
            link(nc.vector.tensor_tensor(hit_a[:], hit_a[:], hit_b[:], ALU.add))
            link(nc.vector.tensor_scalar(bias2[:], cond, biases[:, 3:4], None, ALU.add))
            link(nc.vector.tensor_copy(wr_parts[:, 0:E], wr_raw[:, 0, :]))
            link(nc.vector.tensor_tensor(wr_parts[:, E:2 * E], wr_raw[:, 0, :], wr_parts[:, 0:E].bitcast(F32),
                                         ALU.subtract))

            def first_gate_total(g):
                dve.wait_ge(forget_ready, g.count(1, 1))
                dve.wait_ge(inp_ready, g.count(1, 1))
                if not g.first:
                    dve.wait_ge(log_sum_ready, g.count(1, 0))
                nc.vector.tensor_tensor(gate_sum[:], forget[:], inp[:], ALU.add).then_inc(gate_sum_ready, 1)

            def first_residual1():
                dve.wait_ge(hidden_ready, 1)
                nc.vector.tensor_tensor(x1[0][:], hidden[:], x_all[:, 0:N], ALU.add).then_inc(x1_ready, 1)

            def first_x1_low():
                dve.wait_ge(x1_hi_ready, 1)
                nc.vector.tensor_tensor(x1_lo[0][:], x1[0][:], x1_hi[0][:].bitcast(F32), ALU.subtract)\
                    .then_inc(x1_lo_ready, 1)

            nc.vector.memset(gate_parts[:].bitcast(F32), 0.0).then_inc(consts_ready, 1)
            first_gate_total(Step(0))
            split_x(Step(1))
            dve.wait_ge(kept_counted, 1)
            link(nc.vector.tensor_scalar(all_zero[:], bank[6][:, 0:B], 0.0, None, ALU.is_equal))
            link(nc.vector.tensor_tensor(hit_b[:], all_zero[:], hit_a[:], ALU.mult))
            dve.wait_ge(cond_routed, 1)
            nc.vector.tensor_copy(route_cond[:], bank[7][:, 0:B * E]).then_inc(route_cond_ready, 1)
            nc.vector.tensor_tensor(gain[:], hit_b[:], keep[:], ALU.max).then_inc(keep_ready, 1)
            dve.wait_ge(keep_ready, 3)
            dve.wait_ge(route_cond_ready, 1)
            link(nc.vector.tensor_scalar(gain[:], gain[:], 1.0, None, ALU.add))
            assert setup[0] == SETUP_STEPS
            dve.wait_ge(consts_loaded, 32)
            nc.vector.tensor_copy(eye[:], eye_raw[:]).then_inc(consts_ready, 1)
            dve.wait_ge(sel_cleared, 1)
            nc.vector.tensor_copy(sel[0:2 * E], sel_raw[:]).then_inc(consts_ready, 1)
            dve.wait_ge(consts_ready, 3)
            normalize(Step(0))
            dve.wait_ge(wup_loaded, 64)
            nc.vector.tensor_copy(w_hi[:, WR:BLOCKS, :], w_raw[:, WR:BLOCKS, :]).then_inc(routed_split, 1)
            retention(Step(0))
            split_x(Step(2))
            nc.vector.tensor_copy(w_hi[:, W1:WR, :], w_raw[:, W1:WR, :]).then_inc(shared_split, 1)
            dve.wait_ge(shared_split, 1)
            nc.vector.tensor_tensor(w_lo[:, W1:WR, :], w_raw[:, W1:WR, :], w_hi[:, W1:WR, :].bitcast(F32),
                                    ALU.subtract).then_inc(shared_split, 1)
            scaled_sum(Step(0))
            hidden_state(Step(0))
            first_residual1()
            first_gate_total(Step(1))
            split_x1(Step(0))
            first_x1_low()
            normalize(Step(1))
            route_logits(Step(0))
            dve.wait_ge(down_loaded, 32)
            nc.vector.tensor_copy(down_hi[:], down).then_inc(down_split, 1)
            retention(Step(1))

            def step(g):
                nxt, after_next, prev = g.plus(1), g.plus(2), g.plus(-1)
                early = not after_next.runs
                choose_first(g)
                if early:
                    shared(g, 0)
                choose_second(g)
                if early:
                    shared(g, 1)
                chosen_sum(g)
                if not early:
                    shared(g, 0)
                    shared(g, 1)
                gates_of_chosen(g)
                shared(g, 2)
                shared(g, 3)
                gates_out(g)
                for s in range(HI_ACT, SU):
                    shared_high(g, s)
                if after_next.runs:
                    normalize(after_next)
                if not g.first:
                    mask_z1(prev)
                split_v(g)
                if g.plus(3).runs:
                    split_x(g.plus(3))
                if after_next.runs:
                    retention(after_next)
                for e in range(E):
                    expert(g, e)
                    if e == 2 and nxt.runs:
                        hidden_state(nxt)
                    if e >= 1:
                        low_part(g, e - 1)
                    if e == 0 and nxt.runs:
                        scaled_sum(nxt)
                    if e == 3 and nxt.runs:
                        split_x1(nxt)
                low_part(g, E - 1)
                if nxt.runs:
                    route_logits(nxt)
                residual2(g)

            step(Step(0))
            with dve.Fori(0, TURNS) as turn:
                step(Step(1, turn))
                step(Step(2, turn))
            step(Step(GROUPS - 3))
            step(Step(GROUPS - 2))
            step(Step(GROUPS - 1))
            last = Step(GROUPS - 1)
            dve.wait_ge(x2_hi_ready, GROUPS)
            tt(x2_lo[:], x2[:], x2_hi[:].bitcast(F32), ALU.subtract).then_inc(x2_lo_ready, 1)
            mask_z1(last)
            dve.wait_ge(act2_ready, GROUPS)
            tt(x3[:], x2[:], act2[:], ALU.add).then_inc(x3_ready, 1)
            dve.wait_ge(x3_ready, GROUPS)
            dve.wait_ge(out_stored, 16 * GROUPS)
            tt(seq(out_sb), seq(x3), gain[:, columns(last, GB)].unsqueeze(2).to_broadcast([128, GB, S]), ALU.mult)\
                .then_inc(out_ready, 1)

        @block.tensor
        def _(pe):
            def split_product(out, w, hi, lo, start=True, stop=True):
                nc.tensor.matmul(out, w_hi[:, w, :], hi, start=start, stop=False)
                nc.tensor.matmul(out, w_lo[:, w, :], hi, start=False, stop=False)
                return nc.tensor.matmul(out, w_hi[:, w, :], lo, start=False, stop=stop)

            def gates(g):
                if g.first:
                    pe.wait_ge(w0_split, 2)
                elif g.start <= 2:
                    pe.wait_ge(cand_ready, g.start)
                else:
                    pe.wait_ge(gelu_ready, g.plus(-3).count(E, E))
                pe.wait_ge(x_hi_ready, g.count(1, 1))
                pe.wait_ge(x_lo_ready, g.count(1, 1))
                for n in (WF, WI, WH):
                    split_product(bank[n][:], n, x_hi[:], x_lo[:]).then_inc(gates_mm, 1)

            def route(g):
                pe.wait_ge(x1_hi_ready, g.count(1, 1))
                pe.wait_ge(x1_lo_ready, g.count(1, 1))
                if g.first:
                    pe.wait_ge(route_cond_ready, 1)
                else:
                    pe.wait_ge(gates_T_ready, g.count(1, 0))
                for j in range(GB):
                    hi, lo = (t[g.parity][:, j * S:(j + 1) * S] for t in (x1_hi, x1_lo))
                    nc.tensor.matmul(ROUTE[:, 2 * j * E:2 * (j + 1) * E], hi, wr_parts[:], start=True, stop=False)
                    last = nc.tensor.matmul(ROUTE[:, 2 * j * E:(2 * j + 1) * E], lo, wr_parts[:, 0:E],
                                            start=False, stop=True)
                last.then_inc(route_mm, 1)

            def shared(g):
                if g.first:
                    pe.wait_ge(shared_split, 2)
                for s in range(SU):
                    if s == 0 and not g.first:
                        pe.wait_ge(h_gated_ready, g.count(E, 0))
                    elif s == 1 and not g.first:
                        pe.wait_ge(x2_ready, g.count(1, 0))
                    elif s == 2:
                        if g.plus(2).runs:
                            pe.wait_ge(cand_ready, g.plus(2).count(1, 1))
                        else:
                            pe.wait_ge(gelu_ready, g.count(E, 0))
                    elif s == 3:
                        pe.wait_ge(silu_ready, g.count(SU, 1))
                    hi, lo = x1_hi[g.parity][:], x1_lo[g.parity][:]
                    split_product(PAIRS[s][0][:], W1 + s, hi, lo)
                    split_product(PAIRS[s][1][:], W3 + s, hi, lo).then_inc(shared_mm, 1)

            def transpose_gates(g):
                pe.wait_ge(gate_parts_ready, g.count(1, 1))
                if g.first:
                    pe.wait_ge(consts_ready, 3)
                for j in range(GB):
                    last = nc.tensor.matmul(ROUTE[:, j * S:(j + 1) * S], gate_parts[:, j, :], eye[:],
                                            start=True, stop=True)
                last.then_inc(gates_T_mm, 1)

            def low_rank(g):
                if g.runs:
                    pe.wait_ge(x2_hi_ready, g.count(1, 1))
                    pe.wait_ge(v_lo_ready, g.count(1, 1))
                    if g.plus(1).runs:
                        pe.wait_ge(silu_ready, g.plus(1).count(SU, 2))
                    v = v_parts[:].rearrange("p h k -> p (h k)")
                    nc.tensor.matmul(LOWRANK[:], v, x2_hi[:], start=True, stop=False)
                    pe.wait_ge(x2_lo_ready, g.count(1, 1))
                    nc.tensor.matmul(LOWRANK[:], v, x2_lo[:], start=False, stop=True).then_inc(z1_mm, 1)

            def linear(g):
                if g.runs:
                    if g.plus(1).runs:
                        pe.wait_ge(h_shared_ready, g.plus(1).count(SU, 1))
                    split_product(LINEAR[:], WL, x2_hi[:], x2_lo[:], stop=False)
                    pe.wait_ge(z1_ready, g.count(1, 1))
                    pe.wait_ge(u_loaded, g.count(16, 16))
                    nc.tensor.matmul(LINEAR[:], u_in[:], z1[:], start=False, stop=True).then_inc(linear_mm, 1)

            def up(g, e):
                if g.first and e == 0:
                    pe.wait_ge(routed_split, 2)
                if e < 3:
                    pe.wait_ge(h_shared_ready, g.count(SU, 3 if e < 2 else SU))
                else:
                    pe.wait_ge(gelu_ready, g.count(E, e - 2))
                split_product(bank[e % 3][:], WR + e, x1_hi[g.parity][:], x1_lo[g.parity][:]).then_inc(expert_mm, 1)

            def spread_gate(g, e):
                if e == 0:
                    pe.wait_ge(gates_T_ready, g.count(1, 1))
                if e == 1 and not g.first:
                    pe.wait_ge(z1_ready, g.count(1, 0))
                if e >= 2:
                    pe.wait_ge(h_gated_ready, g.count(E, e - 1))
                nc.tensor.matmul(GATE[e % 2][:], sel[:, e, :], gates_T[:], start=True, stop=True).then_inc(gate_mm, 1)

            def split_down(n, hi, lo, wait_lo, start=False, stop=False):
                nc.tensor.matmul(ACC[:], down_hi[:, n, :], hi, start=start, stop=False)
                nc.tensor.matmul(ACC[:], down_lo[:, n, :], hi, start=False, stop=False)
                wait_lo()
                return nc.tensor.matmul(ACC[:], down_hi[:, n, :], lo, start=False, stop=stop)

            def shared_down(g, s):
                if g.first and s == 0:
                    pe.wait_ge(down_split, 2)
                if s == 0:
                    pe.wait_ge(h_shared_ready, g.count(SU, 2))
                wait_shared_hi(pe, g, s)
                split_down(s, shared_hi[:, s, :], shared_lo[:, s, :],
                           lambda: pe.wait_ge(shared_lo_ready, g.count(SU, s + 1)), start=(s == 0))

            def expert_down(g, e):
                pe.wait_ge(h_hi_ready, g.count(E, e + 1))
                split_down(SU + e, h_hi[e % 4][:], h_lo[e % 4][:], lambda: wait_h_lo(pe, g, e), stop=(e == E - 1))\
                    .then_inc(down_mm, 1)

            def step(g):
                prev = g.plus(-1)
                if g.plus(2).runs:
                    gates(g.plus(2))
                if g.first:
                    route(g)
                shared(g)
                if not g.first:
                    low_rank(prev)
                shared_down(g, 0)
                if not g.plus(2).runs:
                    shared_down(g, 1)
                transpose_gates(g)
                up(g, 0)
                up(g, 1)
                if g.plus(2).runs:
                    shared_down(g, 1)
                up(g, 2)
                spread_gate(g, 0)
                if not g.first:
                    linear(prev)
                spread_gate(g, 1)
                shared_down(g, 2)
                shared_down(g, 3)
                for e in range(E):
                    if e + 3 < E:
                        up(g, e + 3)
                    if e + 2 < E:
                        spread_gate(g, e + 2)
                    if e == E - 2 and g.plus(1).runs:
                        route(g.plus(1))
                    if e >= 1:
                        expert_down(g, e - 1)
                expert_down(g, E - 1)

            def keep_clock(n):
                for _ in range(n):
                    nc.tensor.matmul(bank[6][:, 0:128], ones[:], ones[:], start=True, stop=True)

            pe.wait_ge(ones_ready, 1)
            keep_clock(11)
            gates(Step(0))
            pe.wait_ge(keep_ready, 2)
            nc.tensor.matmul(bank[6][:, 0:B], ones[:], keep[:], start=True, stop=True).then_inc(kept_counted, 1)
            nc.tensor.matmul(bank[7][:, 0:B * E], ones[:], cond_weight[:].rearrange("p b e -> p (b e)"),
                             start=True, stop=True).then_inc(cond_routed, 1)
            gates(Step(1))
            pe.wait_ge(route_cond_ready, 1)
            keep_clock(22)
            step(Step(0))
            with pe.Fori(0, TURNS) as turn:
                step(Step(1, turn))
                step(Step(2, turn))
            step(Step(GROUPS - 3))
            step(Step(GROUPS - 2))
            step(Step(GROUPS - 1))
            keep_clock(8)
            low_rank(Step(GROUPS - 1))
            linear(Step(GROUPS - 1))


_OUT = (D, B * S)


def kernel(x, cond_1024, fside_Bx1x1024x16_0, itok_B_14_1018, L0_cond_W_f, L0_cond_b_f, L0_cond_W_i, L0_cond_b_i,
           L0_cond_W_h, L0_cond_b_h, L1_cond_W_router, L1_cond_router_bias, L1_cond_s_w1, L1_cond_s_w3, L1_cond_s_w2,
           L1_cond_r_w1, L1_cond_r_w2, L2_cond_W, L2_cond_fc_bias):
    import numpy as np
    import concourse.bacc as bacc
    from concourse.bass_utils import run_bass_kernel_spmd

    def lay(a, *axes):
        a = np.asarray(a)
        return np.ascontiguousarray(a.transpose(*axes) if axes else a)

    fside = np.asarray(fside_Bx1x1024x16_0)
    s_w1, s_w3, s_w2 = (np.asarray(a) for a in (L1_cond_s_w1, L1_cond_s_w3, L1_cond_s_w2))
    f = np.float32
    k = np.arange(128)
    sequence = (k % (GB * R)) // R
    block_mask = np.where(sequence[:, None] == np.arange(N)[None, :] // S, f(1.0 / (D * R)), f(0)).astype(f)
    sel = np.zeros((2 * E, E, 128), f)
    for e in range(E):
        sel[e, e, :] = 1
        sel[E + e, e, :] = 1
    arrays = {
        "xT": lay(np.asarray(x).reshape(B * S, D), 1, 0),
        "small": np.concatenate([
            lay(cond_1024, 1, 0),
            np.stack([np.asarray(a) for a in (L0_cond_b_f, L0_cond_b_i, L0_cond_b_h, L2_cond_fc_bias)], 1),
            lay(np.asarray(L1_cond_W_router).reshape(E, 2, D), 2, 1, 0).reshape(D, 2 * E),
            np.broadcast_to(np.asarray(L1_cond_router_bias), (128, E)),
            np.stack([k, k - D], 1).astype(f),
            np.broadcast_to((E - np.arange(E)).astype(f), (128, E))], 1),
        "fsT": lay(fside[:, 0], 1, 0, 2).reshape(D, B * R),
        "uT": np.tile(lay(fside[:, 0].reshape(GROUPS, GB, D, R), 1, 3, 0, 2).reshape(GB * R, GROUPS * D), (2, 1)),
        "itok": lay(itok_B_14_1018),
        "gatesT": lay(np.stack([np.asarray(a) for a in (L0_cond_W_f, L0_cond_W_i, L0_cond_W_h)]), 2, 0, 1),
        "s1T": lay(s_w1.reshape(SU, 128, D), 2, 0, 1),
        "s3T": lay(s_w3.reshape(SU, 128, D), 2, 0, 1),
        "s2T": lay(s_w2.reshape(SHARED, D, 2, 128), 3, 0, 2, 1).reshape(128, SU, D),
        "r1T": lay(L1_cond_r_w1, 2, 0, 1),
        "r2T": lay(L1_cond_r_w2, 2, 0, 1),
        "wlT": lay(L2_cond_W, 1, 0),
        "c_block": block_mask,
        "c_sel": sel,
        "c_eye": np.eye(128, dtype=f),
    }
    nc = bacc.Bacc("TRN2", target_bir_lowering=False, num_devices=1)
    args = [nc.dram_tensor(f"in_{n}", a.shape, mybir.dt.from_np(a.dtype), kind="ExternalInput").ap()
            for n, a in arrays.items()]
    out = nc.dram_tensor("out_T", _OUT, mybir.dt.float32, kind="ExternalOutput").ap()
    build(nc, *args, out)
    r = run_bass_kernel_spmd(nc, [{f"in_{n}": a for n, a in arrays.items()}], core_ids=[0])
    outT = r.results[0]["out_T"]
    return np.ascontiguousarray(np.asarray(outT).reshape(D, B, S).transpose(1, 2, 0))
```
